# Optimizing a Trainium2 kernel written in Bass

```python
import numpy as np
import jax
import jax.numpy as jnp

def _softmax(x, axis=-1):
    return jax.nn.softmax(x, axis=axis)

def _gelu(x):
    return jax.nn.gelu(x, approximate=True)

def _silu(x):
    return jax.nn.silu(x)

def _sigmoid(x):
    return jax.nn.sigmoid(x)

def _layernorm(x, axis=-1, eps=1e-05):
    m = jnp.mean(x, axis=axis, keepdims=True)
    v = jnp.var(x, axis=axis, keepdims=True)
    return (x - m) / jnp.sqrt(v + eps)

def _scatter_add(tgt, idx, src, axis=0):
    return tgt.at[idx].add(src)

def _segment_sum(src, seg, n):
    return jax.ops.segment_sum(src, seg, n)
kernel_name = 'mk_gnn_preln_d4_gnn_r64_eba649'

def setup_inputs(seed: int=0):
    np.random.seed(seed)
    _w = jnp.asarray

    def _rec_inputs():
        import jax
        import jax.numpy as jnp
        _gk = jax.random.key(seed)
        x = -0.0003713 + 1 * jax.random.normal(jax.random.fold_in(_gk, 1), (100000, 128), jnp.float32)
        src = jax.random.randint(jax.random.fold_in(_gk, 2), (50000,), 0, 100000, jnp.int32)
        dst = jax.random.randint(jax.random.fold_in(_gk, 3), (50000,), 0, 100000, jnp.int32)
        _o = jnp.argsort(dst, stable=True)
        src = src[_o]
        dst = dst[_o]
        edge_weight = jax.random.uniform(jax.random.fold_in(_gk, 13), (50000,), jnp.float32, 0.0, 1)
        return (x, src, dst, edge_weight)
    x, src, dst, edge_weight = _rec_inputs()

    def _L0_gnn_setup():
        import jax, jax.numpy as jnp
        import numpy as np
        N_NODES = 100000
        IN_DIM = 128
        H_DIM = 128
        N_EDGES = 25000
        key = jax.random.key(seed)
        k1, k2, k3, k4, k5 = jax.random.split(key, 5)
        h = jax.random.normal(k1, (N_NODES, IN_DIM), dtype=jnp.float32)
        edge_src = jax.random.randint(k2, (N_EDGES,), 0, N_NODES, dtype=jnp.int64)
        edge_dst = jax.random.randint(k3, (N_EDGES,), 0, N_NODES, dtype=jnp.int64)
        bound = 1.0 / np.sqrt(IN_DIM)
        W = jax.random.uniform(k4, (H_DIM, IN_DIM), minval=-bound, maxval=bound, dtype=jnp.float32)
        b = jax.random.uniform(k5, (H_DIM,), minval=-bound, maxval=bound, dtype=jnp.float32)
        return {'h': h, 'edge_src': edge_src, 'edge_dst': edge_dst, 'W': W, 'b': b}
    _L0_gnn_all = _L0_gnn_setup()
    _L0_gnn_in = {k: v for k, v in _L0_gnn_all.items() if k in ('W', 'b')}
    del _L0_gnn_all

    def _L1_gnn_setup():
        import jax, jax.numpy as jnp
        import numpy as np
        N_NODES = 100000
        N_EDGES = 9375
        DIM = 128
        key = jax.random.key(seed)
        k = jax.random.split(key, 6)
        h = jax.random.normal(k[0], (N_NODES, DIM), dtype=jnp.float32)
        edge_index = jax.random.randint(k[1], (2, N_EDGES), 0, N_NODES, dtype=jnp.int64)
        s = 1.0 / np.sqrt(DIM)
        W_self = jax.random.normal(k[2], (DIM, DIM), dtype=jnp.float32) * s
        b_self = jax.random.normal(k[3], (DIM,), dtype=jnp.float32) * s
        W_nei = jax.random.normal(k[4], (DIM, DIM), dtype=jnp.float32) * s
        b_nei = jax.random.normal(k[5], (DIM,), dtype=jnp.float32) * s
        return {'h': h, 'edge_index': edge_index, 'W_self': W_self, 'b_self': b_self, 'W_nei': W_nei, 'b_nei': b_nei}
    _L1_gnn_all = _L1_gnn_setup()
    _L1_gnn_in = {k: v for k, v in _L1_gnn_all.items() if k in ('W_self', 'b_self', 'W_nei', 'b_nei')}
    del _L1_gnn_all

    def _L2_gnn_setup():
        import jax, jax.numpy as jnp
        import numpy as np
        N_NODES = 100000
        N_EDGES = 25000
        EMB = 128
        key = jax.random.key(seed)
        k1, k2, k3, k4, k5, k6 = jax.random.split(key, 6)
        embeddings = jax.random.normal(k1, (N_NODES, EMB), dtype=jnp.float32)
        edge_row = jax.random.randint(k2, (N_EDGES,), 0, N_NODES, dtype=jnp.int32)
        edge_col = jax.random.randint(k3, (N_EDGES,), 0, N_NODES, dtype=jnp.int32)
        edge_val = jax.random.uniform(k4, (N_EDGES,), dtype=jnp.float32)
        W1 = jax.random.normal(k5, (EMB, EMB), dtype=jnp.float32) * (1.0 / np.sqrt(EMB))
        W2 = jax.random.normal(k6, (EMB, EMB), dtype=jnp.float32) * (1.0 / np.sqrt(EMB))
        return {'embeddings': embeddings, 'edge_row': edge_row, 'edge_col': edge_col, 'edge_val': edge_val, 'W1': W1, 'W2': W2}
    _L2_gnn_all = _L2_gnn_setup()
    _L2_gnn_in = {k: v for k, v in _L2_gnn_all.items() if k in ('W1', 'W2')}
    del _L2_gnn_all

    def _L3_gnn_setup():
        import jax, jax.numpy as jnp
        import numpy as np
        N, E, D = (100000, 9375, 128)
        key = jax.random.key(seed)
        ks = jax.random.split(key, 6)
        s = 1.0 / np.sqrt(D)
        return {'h': jax.random.normal(ks[0], (N, D), dtype=jnp.float32), 'edge_index': jax.random.randint(ks[1], (2, E), 0, N, dtype=jnp.int64), 'Wg': jax.random.normal(ks[2], (2 * D, D), dtype=jnp.float32) * s, 'bg': jnp.zeros((D,), dtype=jnp.float32), 'Ws': jax.random.normal(ks[3], (D, D), dtype=jnp.float32) * s, 'bs': jnp.zeros((D,), dtype=jnp.float32), 'Wr': jax.random.normal(ks[4], (D, D), dtype=jnp.float32) * s, 'br': jnp.zeros((D,), dtype=jnp.float32)}
    _L3_gnn_all = _L3_gnn_setup()
    _L3_gnn_in = {k: v for k, v in _L3_gnn_all.items() if k in ('Wg', 'bg', 'Ws', 'bs', 'Wr', 'br')}
    del _L3_gnn_all
    return {'x': x, 'src': src, 'dst': dst, 'edge_weight': edge_weight, 'L0_gnn_W': _L0_gnn_in['W'], 'L0_gnn_b': _L0_gnn_in['b'], 'L1_gnn_W_self': _L1_gnn_in['W_self'], 'L1_gnn_b_self': _L1_gnn_in['b_self'], 'L1_gnn_W_nei': _L1_gnn_in['W_nei'], 'L1_gnn_b_nei': _L1_gnn_in['b_nei'], 'L2_gnn_W1': _L2_gnn_in['W1'], 'L2_gnn_W2': _L2_gnn_in['W2'], 'L3_gnn_Wg': _L3_gnn_in['Wg'], 'L3_gnn_bg': _L3_gnn_in['bg'], 'L3_gnn_Ws': _L3_gnn_in['Ws'], 'L3_gnn_bs': _L3_gnn_in['bs'], 'L3_gnn_Wr': _L3_gnn_in['Wr'], 'L3_gnn_br': _L3_gnn_in['br']}

def reference(x, src, dst, edge_weight, L0_gnn_W, L0_gnn_b, L1_gnn_W_self, L1_gnn_b_self, L1_gnn_W_nei, L1_gnn_b_nei, L2_gnn_W1, L2_gnn_W2, L3_gnn_Wg, L3_gnn_bg, L3_gnn_Ws, L3_gnn_bs, L3_gnn_Wr, L3_gnn_br):
    import jax
    import jax.numpy as jnp

    def _L0_gnn_ref(h, edge_src, edge_dst, W, b):
        import jax, jax.numpy as jnp
        import numpy as np
        N_NODES = 100000
        IN_DIM = 128
        H_DIM = 128
        N_EDGES = 25000
        agg = jax.ops.segment_sum(h[edge_src], edge_dst, num_segments=N_NODES)
        return agg @ W.T + b

    def _L1_gnn_ref(h, edge_index, W_self, b_self, W_nei, b_nei):
        import jax, jax.numpy as jnp
        import numpy as np
        N_NODES = 100000
        N_EDGES = 9375
        DIM = 128
        src, dst = (edge_index[0], edge_index[1])
        n = h.shape[0]
        msgs = h[src]
        agg = jax.ops.segment_sum(msgs, dst, num_segments=n)
        deg = jax.ops.segment_sum(jnp.ones_like(dst, dtype=h.dtype), dst, num_segments=n)
        deg = jnp.clip(deg, 1.0, None)[:, None]
        mean = agg / deg
        out = h @ W_self.T + b_self + mean @ W_nei.T + b_nei
        return jax.nn.relu(out)

    def _L2_gnn_ref(embeddings, edge_row, edge_col, edge_val, W1, W2):
        import jax, jax.numpy as jnp
        import numpy as np
        N_NODES = 100000
        N_EDGES = 25000
        EMB = 128
        gathered = embeddings[edge_col] * edge_val[:, None]
        relevant = jax.ops.segment_sum(gathered, edge_row, num_segments=N_NODES)
        non_interactive = relevant @ W1
        interactive = relevant * embeddings @ W2
        return non_interactive + interactive

    def _L3_gnn_ref(h, edge_index, Wg, bg, Ws, bs, Wr, br):
        import jax, jax.numpy as jnp
        import numpy as np
        N, E, D = (100000, 9375, 128)
        send, rec = (edge_index[0], edge_index[1])
        h_rec = h[rec]
        h_send = h[send]
        gate_in = h_rec @ Wg[:h.shape[1]] + h_send @ Wg[h.shape[1]:] + bg
        eta = jax.nn.sigmoid(gate_in)
        h_messages = eta * (h_send @ Ws + bs)
        h_agg = jax.ops.segment_sum(h_messages, rec, num_segments=h.shape[0])
        return h @ Wr + br + h_agg
    edge_index = jnp.stack([src, dst])
    h = jnp.maximum(_layernorm(x, axis=-1), 0.0)
    x = x + _L0_gnn_ref(h, src, dst, L0_gnn_W, L0_gnn_b)
    h = jnp.maximum(_layernorm(x, axis=-1), 0.0)
    x = x + _L1_gnn_ref(h, edge_index, L1_gnn_W_self, L1_gnn_b_self, L1_gnn_W_nei, L1_gnn_b_nei)
    h = jnp.maximum(_layernorm(x, axis=-1), 0.0)
    x = x + _L2_gnn_ref(h, src, dst, edge_weight, L2_gnn_W1, L2_gnn_W2)
    h = jnp.maximum(_layernorm(x, axis=-1), 0.0)
    x = x + _L3_gnn_ref(h, edge_index, L3_gnn_Wg, L3_gnn_bg, L3_gnn_Ws, L3_gnn_bs, L3_gnn_Wr, L3_gnn_br)
    return x

_drawn_inputs = setup_inputs


def setup_inputs(seed=0):
    import zlib

    import numpy as np

    out = dict(_drawn_inputs(seed))
    spreads = {'L3_gnn_bg': (0.0, 0.8), 'L3_gnn_bs': (0.0, 0.307), 'L3_gnn_br': (0.0, 0.1)}
    factors = {}
    for name, (base, spread) in spreads.items():
        noise = np.random.default_rng([zlib.crc32(name.encode()), seed]).standard_normal(out[name].shape)
        drawn = base * np.exp(spread * noise) if base else spread * noise
        out[name] = jnp.asarray(drawn.astype(out[name].dtype))
    for name, factor in factors.items():
        out[name] = (out[name] * factor).astype(out[name].dtype)
    return out
```

```python
from contextlib import ExitStack

import numpy as np

import concourse.bass as bass
from concourse import mybir

F32 = mybir.dt.float32
BF16 = mybir.dt.bfloat16
I32 = mybir.dt.int32
ALU = mybir.AluOpType
ACT = mybir.ActivationFunctionType
AX = mybir.AxisListType

P = 128
NODES = 100000
EDGES = 50000
EPS = 1e-5
WIN = 160
NW = 4
BATCH = WIN * NW
NT = BATCH // P
BATCHES = -(-NODES // BATCH)
PADDED = BATCHES * BATCH
TAIL = NODES - (BATCHES - 1) * BATCH
CAP = 125
EROWS = EDGES // CAP
COLS = 400
HALO = CAP
SPAN = COLS + 2 * HALO
WINDOWS = 640
GROUPS = WINDOWS // P
HI = WINDOWS // 32
SLOTS = 4
ROW = P + 3
INV, NMEAN, NMI = P, P + 1, P + 2
PARAMS = 20
SRC, DST, LOC, DEG, EWT = 0, 4, 8, 12, 16
TILES = EDGES // CAP
TRASH = PADDED
SUM = P + 1
NOWHERE = -4096.0


def settle(eng, moved):
    eng.sem_inc(moved, 1)


class Batch:

    def __init__(self, i, c):
        self.i, self.c = i, c
        self.n = SLOTS * i + c
        self.slot = c % SLOTS
        self.lap = i + c // SLOTS

    def back(self, k):
        return Batch(self.i, self.c - k)

    @property
    def before(self):
        return isinstance(self.n, int) and self.n < 0

    @property
    def real(self):
        return not isinstance(self.n, int) or 0 <= self.n < BATCHES


class Event:

    def __init__(self, sem, layers, moved):
        self.sem, self.layers, self.moved = sem, layers, moved

    def wait(self, eng, layer, b):
        if not b.before:
            base = BATCHES * sum(l < layer for l in self.layers)
            eng.wait_ge(self.sem, base + b.n + 1)
            if eng.engine == mybir.EngineType.SP and not isinstance(b.n, int):
                settle(eng, self.moved)


class Landed:

    def __init__(self, sems, per, moved):
        self.sems, self.per, self.moved = sems, per, moved

    def wait(self, eng, layer, b):
        if not b.before:
            laps = len(range(b.slot, BATCHES, SLOTS))
            base = sum(v for l, v in self.per.items() if l < layer) * laps
            eng.wait_ge(self.sems[b.slot], base + self.per[layer] * (b.lap + 1))
            if eng.engine == mybir.EngineType.SP and not isinstance(b.n, int):
                settle(eng, self.moved)

    def all(self, eng, layer):
        for s in range(SLOTS):
            last = Batch(0, range(s, BATCHES, SLOTS)[-1])
            last.slot, last.lap = s, last.n // SLOTS
            self.wait(eng, layer, last)


def steps(eng, depth, body):
    first = -(-depth // SLOTS) + 1
    last = (BATCHES - 1) // SLOTS
    for i in range(first):
        for u in range(SLOTS):
            body(Batch(i, u))
    with eng.Fori(first, last) as i:
        for u in range(SLOTS):
            body(Batch(i, u))
    for t in range(last * SLOTS, BATCHES + depth):
        body(Batch(t // SLOTS, t % SLOTS))


def build(nc, x, src, dst, edge_weight, W0, b0, W_self, b_self, W_nei, b_nei, W1, W2,
          Wg, bg, Ws, bs, Wr, br, out):
    ctx = ExitStack()
    early = ExitStack()
    with ctx:
        def sem(name):
            return ctx.enter_context(nc.semaphore(name))

        def sb(name, shape, dt=F32, of=ctx):
            return of.enter_context(nc.sbuf_tensor(name, shape, dt))

        def dram(name, shape, dt=F32):
            return nc.dram_tensor(name, shape, dt, kind="Internal").ap()

        nodes = [x, dram("x1", [PADDED, ROW]), dram("x2", [PADDED, ROW]), dram("x3", [PADDED, ROW])]
        sums = dram("sums", [PADDED + P, SUM])
        inv_dram = dram("inv_dram", [EDGES])
        low_dram = dram("low_dram", [WINDOWS])

        ident = sb("ident", [P, P])
        iota_win = sb("iota_win", [P, NW, WIN])
        iota_pair = sb("iota_pair", [P, NW, 2 * P])
        params = sb("params", [P, BATCHES + 3, PARAMS], I32)
        flag = sb("flag", [1, 1], I32)
        g_earlier = sb("g_earlier", [CAP, CAP])
        g_trash = sb("g_trash", [CAP, 1])
        g_ones = sb("g_ones", [CAP, CAP])
        g_msg = sb("g_msg", [CAP, SUM])
        g_zero = sb("g_zero", [P, NT * SUM])
        edges = sb("edges", [CAP, COLS, 3], I32)
        w0t = sb("w0t", [P, P])
        wselft = sb("wselft", [P, P])
        wneit = sb("wneit", [P, P])
        w1 = sb("w1", [P, P])
        w2 = sb("w2", [P, P])
        wg_rec = sb("wg_rec", [P, P])
        wg_ws = sb("wg_ws", [P, 2 * P])
        wr = sb("wr", [P, P])
        eps_col = sb("eps_col", [P, 1])
        ones3 = sb("ones3", [3, P], BF16)
        bias0 = sb("bias0", [3, 4, P], BF16)
        bias1 = sb("bias1", [3, 4, P], BF16)
        bias3 = sb("bias3", [3, 4, P], BF16)
        biase = sb("biase", [3, 4, P], BF16)

        def pre(name, shape, dt=F32):
            return sb(name, shape, dt, early)

        dst_halo = pre("dst_halo", [CAP, SPAN], I32)
        dstf = pre("dstf", [CAP, SPAN])
        same = pre("same", [CAP, SPAN + 1])
        ones_row = pre("ones_row", [CAP, SPAN])
        fwd = pre("fwd", [CAP, SPAN])
        bwd = pre("bwd", [CAP, SPAN])
        inv_deg = pre("inv_deg", [CAP, COLS])
        falls = pre("falls", [CAP, COLS])
        bad = pre("bad", [CAP, 1])
        wid = pre("wid", [CAP, COLS], I32)
        wid_hi = pre("wid_hi", [CAP, COLS], I32)
        wid_lo = pre("wid_lo", [CAP, COLS], I32)
        iota32 = pre("iota32", [CAP, 32])
        is_hi = pre("is_hi", [CAP, COLS, HI], BF16)
        is_lo = pre("is_lo", [CAP, COLS, 32], BF16)
        count = pre("count", [HI, 32])
        upto = pre("upto", [HI, 32])
        low = pre("low", [HI, 32])
        over = pre("over", [HI, 32])
        bad_hi = pre("bad_hi", [HI, 1])
        rows_up = pre("rows_up", [HI, HI])
        ones_col = pre("ones_col", [P, 1])
        low_w = pre("low_w", [P, GROUPS])
        row0 = pre("row0", [P, GROUPS], I32)
        row0f = pre("row0f", [P, GROUPS])
        start = pre("start", [P, GROUPS])
        row1 = pre("row1", [P, GROUPS], I32)
        iota_slot = pre("iota_slot", [P, CAP])
        in0 = pre("in0", [P, GROUPS, CAP])
        in1 = pre("in1", [P, GROUPS, CAP])
        fetched_i = pre("fetched_i", [P, 2, 2, GROUPS, CAP], I32)
        fetched_f = pre("fetched_f", [P, 2, 2, GROUPS, CAP])
        part = pre("part", [P, 2, GROUPS, CAP])
        table = pre("table", [P, 4, GROUPS, CAP])
        win_base = pre("win_base", [P, WINDOWS])
        dtab = pre("dtab", [P, WINDOWS])
        inside = pre("inside", [P, WINDOWS])
        w_raw = pre("w_raw", [P, 3, P])
        b_raw = pre("b_raw", [3, 6, P])
        b_sum = pre("b_sum", [3, P])
        b_hi = pre("b_hi", [3, 6, P], BF16)
        b_mid = pre("b_mid", [3, 6, P], BF16)
        b_lo = pre("b_lo", [3, 6, P], BF16)
        b_r1 = pre("b_r1", [3, 6, P])
        b_r2 = pre("b_r2", [3, 6, P])
        b_mix = pre("b_mix", [3, 2, 6, P])
        src_raw = pre("src_raw", [CAP, COLS], I32)
        ew_raw = pre("ew_raw", [CAP, COLS], I32)
        early.close()

        ep = sb("ep", [P, SLOTS, PARAMS], I32)
        rows = sb("rows", [P, SLOTS, 2 * NW, ROW])
        xn = sb("xn", [P, SLOTS, NT, ROW])
        xo = sb("xo", [P, SLOTS, NT, ROW])
        xh = sb("xh", [P, SLOTS, NT, P])
        sel = sb("sel", [P, SLOTS, NW * 2 * P])
        msg = sb("msg", [P, SLOTS, NW, P])
        scale = sb("scale", [P, SLOTS, NW])
        agg_t = sb("agg_t", [P, SLOTS, BATCH])
        h_t = sb("h_t", [P, SLOTS, BATCH])
        prod_t = sb("prod_t", [P, SLOTS, BATCH])
        eh = sb("eh", [P, SLOTS, 2 * NW, P])
        eh_t = sb("eh_t", [P, 2, 2 * NW, P])
        eta = sb("eta", [P, 2, NW, P])
        stat = sb("stat", [P, SLOTS, NT, 6])
        var = sb("var", [P, SLOTS, NT, 2])
        std = sb("std", [P, SLOTS, NT])
        estat = sb("estat", [P, SLOTS, NW, 6])
        evar = sb("evar", [P, SLOTS, NW, 2])
        estd = sb("estd", [P, SLOTS, NW])
        einv = sb("einv", [P, SLOTS, NW])
        enmi = sb("enmi", [P, SLOTS, NW])

        g_edge = sb("g_edge", [CAP, 3], I32)
        g_key = sb("g_key", [CAP, 1])
        g_diag = sb("g_diag", [CAP, CAP])
        g_same = sb("g_same", [CAP, CAP])
        g_before = sb("g_before", [CAP, CAP])
        g_prior = sb("g_prior", [CAP, 1])
        g_tof = sb("g_tof", [CAP, 1])
        g_to = sb("g_to", [CAP, 1], I32)
        g_total = sb("g_total", [CAP, SUM])
        g_sums = sb("g_sums", [P, NT, SUM])
        g_deg = sb("g_deg", [P, NT])
        g_mean = sb("g_mean", [P, NT, P])

        ps_e = ctx.enter_context(nc.psum_tensor("ps_e", [P, 1024], F32))
        ps_t = ctx.enter_context(nc.psum_tensor("ps_t", [P, 1024], F32))
        ps_o = ctx.enter_context(nc.psum_tensor("ps_o", [P, 2, 1024], F32))

        joined = sem("joined")
        moved = sem("moved")
        ALL = (0, 1, 3)

        def ev(name, layers=ALL):
            return Event(sem(name), [l for l in layers if l in ALL], moved)

        def landed(name, per):
            return Landed([sem(f"{name}{s}") for s in range(SLOTS)], {l: v for l, v in per.items() if l in ALL}, moved)

        ep_in = landed("ep_in", {l: 16 for l in ALL})
        gathered = landed("gathered", {0: 64, 1: 64, 2: 64, 3: 128})
        x_in = landed("x_in", {l: 16 for l in ALL})
        x_stored = landed("x_stored", {l: 16 for l in ALL})
        x_tail = sem("x_tail")
        out_tail = sem("out_tail")
        e_stats = ev("e_stats", (0,))
        e_var = ev("e_var", (0,))
        e_std = ev("e_std", (0,))
        e_inv = ev("e_inv", (0,))
        e_nmi = ev("e_nmi", (0,))
        e_scale = ev("e_scale", (1, 2))
        e_norm = ev("e_norm")
        e_normd = ev("e_normd", (3,))
        e_sel = ev("e_sel")
        e_tr = ev("e_tr", (3,))
        e_ht = ev("e_ht", (3,))
        e_gate = ev("e_gate", (3,))
        e_eta = ev("e_eta", (3,))
        e_msg = ev("e_msg", (3,))
        e_agg = ev("e_agg", (0, 1, 2))
        n_aggt = ev("n_aggt", (0, 1, 2))
        n_norm = ev("n_norm", (1, 2, 3))
        n_tr = ev("n_tr", (1, 2, 3))
        n_ht = ev("n_ht", (1, 3))
        n_prod = ev("n_prod", (2,))
        n_mm = ev("n_mm")
        n_out = ev("n_out")
        n_stats = ev("n_stats", (0, 1, 2))
        n_aggr = ev("n_aggr", (0, 1, 2))
        n_var = ev("n_var", (0, 1, 2))
        n_std = ev("n_std", (0, 1, 2))
        n_inv = ev("n_inv", (0, 1, 2))
        n_fin = ev("n_fin", (0, 1, 2))

        g_edge_in = sem("g_edge_in")
        g_rows_in = sem("g_rows_in")
        g_zeroed = sem("g_zeroed")
        g_added = sem("g_added")
        g_diagd = sem("g_diagd")
        g_keys = sem("g_keys")
        g_var = sem("g_var")
        g_std = sem("g_std")
        g_hd = sem("g_hd")
        g_tr = sem("g_tr")
        g_ht = sem("g_ht")
        g_gate = sem("g_gate")
        g_eta = sem("g_eta")
        g_msgd = sem("g_msgd")
        g_comb = sem("g_comb")
        g_totald = sem("g_totald")
        g_step = sem("g_step")
        gn_in = sem("gn_in")
        gn_sums_in = sem("gn_sums_in")
        gn_stored = sem("gn_stored")
        gn_var = sem("gn_var")
        gn_std = sem("gn_std")
        gn_ready = sem("gn_ready")
        gn_tr = sem("gn_tr")
        gn_take = sem("gn_take")
        gn_prod = sem("gn_prod")
        gn_mm = sem("gn_mm")
        gn_out = sem("gn_out")
        gn_step = sem("gn_step")

        def join(eng, k):
            eng.drain().then_inc(joined, 1)
            eng.wait_ge(joined, 5 * k)

        p_in = sem("p_in")
        p_rows = sem("p_rows")
        p_dst = [sem("p_dst0"), sem("p_dst1"), sem("p_dst2")]
        p_w = sem("p_w")
        p_raw = sem("p_raw")
        p_halo = sem("p_halo")
        p_inv = sem("p_inv")
        p_invd = sem("p_invd")
        p_low = sem("p_low")
        p_lowd = sem("p_lowd")
        p_lowin = sem("p_lowin")
        p_pool = sem("p_pool")
        p_sel = sem("p_sel")
        p_fetch = sem("p_fetch")
        p_onehot = sem("p_onehot")
        p_count = sem("p_count")
        p_upto = sem("p_upto")
        p_rank = sem("p_rank")
        p_wt = sem("p_wt")
        p_wtc = sem("p_wtc")
        p_tab = sem("p_tab")
        p_tabt = sem("p_tabt")
        p_tabc = sem("p_tabc")
        p_step = sem("p_step")

        dst_rows = dst.rearrange("(p c) -> p c", c=COLS)
        edge_rows = [src.rearrange("(r c) -> r c", c=CAP), dst.rearrange("(r c) -> r c", c=CAP),
                     edge_weight.rearrange("(r c) -> r c", c=CAP), inv_dram.rearrange("(r c) -> r c", c=CAP)]

        def sp_prepare(sp):
            sp.dma_start(dst_halo[:, HALO:HALO + COLS], dst_rows).then_inc(p_dst[0], 16)
            sp.wait_ge(p_halo, 1)
            sp.dma_start(dst_halo[1:CAP, 0:HALO], dst_rows[0:CAP - 1, COLS - HALO:COLS]).then_inc(p_dst[1], 16)
            sp.dma_start(dst_halo[0:CAP - 1, HALO + COLS:SPAN], dst_rows[1:CAP, 0:HALO]).then_inc(p_dst[2], 16)
            sp.dma_start(src_raw[:], src.rearrange("(p c) -> p c", c=COLS)).then_inc(p_raw, 16)
            sp.dma_start(ew_raw[:], edge_weight.bitcast(I32).rearrange("(p c) -> p c", c=COLS)).then_inc(p_raw, 16)
            for k, w in enumerate((W0, W_self, W_nei)):
                sp.dma_start(w_raw[:, k, :], w).then_inc(p_w, 16)
            sp.dma_start(w1[:], W1).then_inc(p_w, 16)
            sp.dma_start(w2[:], W2).then_inc(p_w, 16)
            sp.dma_start(wg_rec[:], Wg[0:P, :]).then_inc(p_w, 16)
            sp.dma_start(wg_ws[:, 0:P], Wg[P:2 * P, :]).then_inc(p_w, 16)
            sp.dma_start(wg_ws[:, P:2 * P], Ws).then_inc(p_w, 16)
            sp.dma_start(wr[:], Wr).then_inc(p_w, 16)
            for k, b in enumerate((b0, b_self, b_nei, bg, bs, br)):
                one = b.rearrange("(a f) -> a f", a=1)
                for q in range(3):
                    sp.dma_start(b_raw[q:q + 1, k, :], one).then_inc(p_w, 16)
            sp.wait_ge(p_inv, 1)
            sp.dma_start(inv_dram.rearrange("(p c) -> p c", c=COLS), inv_deg[:]).then_inc(p_invd, 16)
            sp.wait_ge(p_low, 1)
            sp.dma_start(low_dram.rearrange("(h l) -> h l", l=32), low[:]).then_inc(p_lowd, 16)
            sp.wait_ge(p_lowd, 16)
            with nc.allow_non_contiguous_dma(reason="640 words once"):
                sp.dma_start(low_w[:], low_dram.rearrange("(g p) -> p g", p=P)).then_inc(p_lowin, 16)
            sp.wait_ge(p_lowin, 16)
            sp.wait_ge(p_invd, 16)
            sp.wait_ge(p_w, 16 * 27)

        def pool_prepare(pool):
            g = nc.gpsimd
            g.memset(ident[:], 0.0).then_inc(p_pool, 1)
            pool.wait_ge(p_pool, 1)
            g.affine_select(out=ident[:], in_=ident[:], compare_op=ALU.not_equal, fill=1.0, base=0,
                            pattern=[[-1, P]], channel_multiplier=1).then_inc(p_pool, 1)
            g.iota(iota_win[:], pattern=[[0, NW], [1, WIN]], base=0, channel_multiplier=0,
                   allow_small_or_imprecise_dtypes=True).then_inc(p_pool, 1)
            g.iota(iota_pair[:], pattern=[[P - WIN, NW], [1, 2 * P]], base=0, channel_multiplier=0,
                   allow_small_or_imprecise_dtypes=True).then_inc(p_pool, 1)
            g.iota(iota32[:], pattern=[[1, 32]], base=0, channel_multiplier=0,
                   allow_small_or_imprecise_dtypes=True).then_inc(p_pool, 1)
            g.iota(iota_slot[:], pattern=[[1, CAP]], base=0, channel_multiplier=0,
                   allow_small_or_imprecise_dtypes=True).then_inc(p_pool, 1)
            g.iota(win_base[:], pattern=[[WIN, WINDOWS]], base=0, channel_multiplier=0,
                   allow_small_or_imprecise_dtypes=True).then_inc(p_pool, 1)
            g.memset(rows_up[:], 1.0).then_inc(p_pool, 1)
            g.iota(g_trash[:], pattern=[[0, 1]], base=TRASH, channel_multiplier=1,
                   allow_small_or_imprecise_dtypes=True).then_inc(p_pool, 1)
            g.memset(g_earlier[:], 1.0).then_inc(p_pool, 1)
            pool.wait_ge(p_pool, 10)
            g.affine_select(out=g_earlier[:], in_=g_earlier[:], compare_op=ALU.is_gt, fill=0.0, base=0,
                            pattern=[[-1, CAP]], channel_multiplier=1).then_inc(p_pool, 1)
            g.affine_select(out=rows_up[:], in_=rows_up[:], compare_op=ALU.is_gt, fill=0.0, base=0,
                            pattern=[[1, HI]], channel_multiplier=-1).then_inc(p_pool, 1)
            pool.wait_ge(p_rows, 1)
            for f in range(3):
                to = fetched_i[:, f] if f < 2 else fetched_f[:, 0]
                for k, at in enumerate((row0, row1)):
                    for q in range(GROUPS):
                        g.indirect_dma_start(to[:, k, q, :], None, edge_rows[f], bass.IndirectOffsetOnAxis(
                            ap=at[:, q:q + 1], axis=0)).then_inc(p_fetch, 16)
            pool.wait_ge(p_invd, 16)
            for k, at in enumerate((row0, row1)):
                for q in range(GROUPS):
                    g.indirect_dma_start(fetched_f[:, 1, k, q, :], None, edge_rows[3], bass.IndirectOffsetOnAxis(
                        ap=at[:, q:q + 1], axis=0)).then_inc(p_fetch, 16)

        def act_prepare(act):
            pass

        def pe_prepare(pe):
            pe.wait_ge(p_pool, 12)
            pe.wait_ge(p_w, 16 * 27)
            for k in range(3):
                mm = pe.transpose(ps_t[:, k * P:(k + 1) * P], w_raw[:, k, :], ident[:])
            mm.then_inc(p_wt, 1)
            pe.wait_ge(p_onehot, 2)
            for c in range(COLS):
                mm = pe.matmul(ps_o[0:HI, 0, 0:32], is_hi[:, c, :], is_lo[:, c, :], start=(c == 0), stop=(c == COLS - 1))
            mm.then_inc(p_count, 1)
            pe.wait_ge(p_upto, 1)
            pe.matmul(ps_o[0:HI, 1, 0:1], rows_up[:], upto[:, 31:32], start=True, stop=True).then_inc(p_rank, 1)
            pe.wait_ge(p_upto, 2)
            pe.matmul(ps_o[0:1, 1, 512:513], bad[:], ones_col[0:CAP, :], start=True, stop=False)
            pe.matmul(ps_o[0:1, 1, 512:513], bad_hi[:], ones_col[0:HI, :], start=False, stop=True).then_inc(p_rank, 1)
            for f in range(4):
                pe.wait_ge(p_tab, f + 1)
                if f:
                    pe.wait_ge(p_tabc, f)
                for q in range(GROUPS):
                    mm = pe.transpose(ps_t[0:CAP, q * P:(q + 1) * P], table[:, f, q, :], ident[:])
                mm.then_inc(p_tabt, 1)

        def dve_prepare(dve):
            v = nc.vector
            n = [0]

            def done(ins):
                n[0] += 1
                ins.then_inc(p_step, 1)
                dve.wait_ge(p_step, n[0])

            v.memset(dst_halo[:, 0:HALO], -1)
            v.memset(dst_halo[:, HALO + COLS:SPAN], 1 << 20).then_inc(p_halo, 1)
            v.memset(eps_col[:], EPS)
            v.memset(ones3[:], 1.0)
            v.memset(ones_col[:], 1.0)
            v.memset(same[:], 0.0)
            v.memset(params[:], 0)
            done(v.memset(ones_row[:], 1.0))
            v.memset(g_ones[:], 1.0)
            v.memset(g_msg[:], 1.0)
            v.memset(g_zero[:], 0.0)
            for s in p_dst:
                dve.wait_ge(s, 16)
            v.tensor_copy(edges[:, :, 1], dst_halo[:, HALO:HALO + COLS])
            dve.wait_ge(p_raw, 32)
            v.tensor_copy(edges[:, :, 0], src_raw[:])
            v.tensor_copy(edges[:, :, 2], ew_raw[:])
            done(v.tensor_copy(dstf[:], dst_halo[:]))
            done(v.tensor_tensor(same[:, 1:SPAN], dstf[:, 1:SPAN], dstf[:, 0:SPAN - 1], ALU.is_equal))
            v.tensor_tensor_scan(fwd[:], same[:, 0:SPAN], ones_row[:], 0.0, ALU.mult, ALU.add)
            done(v.tensor_tensor_scan(bwd[:, ::-1], same[:, 1:SPAN + 1][:, ::-1], ones_row[:], 0.0, ALU.mult, ALU.add))
            done(v.scalar_tensor_tensor(out=inv_deg[:], in0=fwd[:, HALO:HALO + COLS], scalar=-1.0,
                                        in1=bwd[:, HALO:HALO + COLS], op0=ALU.add, op1=ALU.add))
            v.reciprocal(inv_deg[:], inv_deg[:]).then_inc(p_inv, 1)
            done(v.tensor_tensor(falls[:], dstf[:, HALO:HALO + COLS], dstf[:, HALO - 1:HALO + COLS - 1], ALU.is_lt))
            v.tensor_reduce(bad[:], falls[:], AX.X, ALU.max)
            done(v.tensor_scalar(wid[:], dst_halo[:, HALO:HALO + COLS], 5, None, ALU.arith_shift_right))
            done(v.tensor_scalar(wid_hi[:], wid[:], 0.2, -0.4, ALU.mult, ALU.add))
            v.tensor_scalar(wid_lo[:], wid_hi[:], 31, None, ALU.bitwise_and)
            done(v.tensor_scalar(wid[:], wid_hi[:], 5, None, ALU.arith_shift_right))
            dve.wait_ge(p_pool, 12)
            v.tensor_tensor(is_hi[:], wid[:].rearrange("p (c a) -> p c a", a=1).to_broadcast([CAP, COLS, HI]),
                            iota32[:, 0:HI].rearrange("p (a h) -> p a h", a=1).to_broadcast([CAP, COLS, HI]),
                            ALU.is_equal).then_inc(p_onehot, 1)
            v.tensor_tensor(is_lo[:], wid_lo[:].rearrange("p (c a) -> p c a", a=1).to_broadcast([CAP, COLS, 32]),
                            iota32[:].rearrange("p (a h) -> p a h", a=1).to_broadcast([CAP, COLS, 32]),
                            ALU.is_equal).then_inc(p_onehot, 1)
            dve.wait_ge(p_w, 16 * 27)
            done(v.tensor_tensor(b_sum[:], b_raw[:, 1, :], b_raw[:, 2, :], ALU.add))
            done(v.tensor_copy(b_raw[:, 1, :], b_sum[:]))
            done(v.tensor_copy(b_hi[:], b_raw[:]))
            done(v.tensor_tensor(b_r1[:], b_raw[:], b_hi[:], ALU.subtract))
            done(v.tensor_copy(b_mid[:], b_r1[:]))
            done(v.tensor_tensor(b_r2[:], b_r1[:], b_mid[:], ALU.subtract))
            done(v.tensor_copy(b_lo[:], b_r2[:]))
            done(v.tensor_scalar(b_mix[:, 0], b_hi[:], ident[0:3, 0:1], None, ALU.mult))
            done(v.scalar_tensor_tensor(out=b_mix[:, 1], in0=b_mid[:], scalar=ident[0:3, 1:2], in1=b_mix[:, 0],
                                        op0=ALU.mult, op1=ALU.add))
            done(v.scalar_tensor_tensor(out=b_mix[:, 0], in0=b_lo[:], scalar=ident[0:3, 2:3], in1=b_mix[:, 1],
                                        op0=ALU.mult, op1=ALU.add))
            for q in range(4):
                v.tensor_copy(bias0[:, q, :], b_mix[:, 0, 0, :])
                v.tensor_copy(bias1[:, q, :], b_mix[:, 0, 1, :])
                v.tensor_copy(biase[:, q, :], b_mix[:, 0, 3 + q % 2, :])
                v.tensor_copy(bias3[:, q, :], b_mix[:, 0, 5, :])
            dve.wait_ge(p_wt, 1)
            v.tensor_copy(w0t[:], ps_t[:, 0:P])
            v.tensor_copy(wselft[:], ps_t[:, P:2 * P])
            done(v.tensor_copy(wneit[:], ps_t[:, 2 * P:3 * P]))
            dve.wait_ge(p_count, 1)
            done(v.tensor_copy(count[:], ps_o[0:HI, 0, 0:32]))
            v.tensor_tensor_scan(upto[:], ones_row[0:HI, 0:32], count[:], 0.0, ALU.mult, ALU.add).then_inc(p_upto, 1)
            done(v.tensor_scalar(over[:], count[:], float(CAP), None, ALU.is_gt))
            done(v.tensor_reduce(bad_hi[:], over[:], AX.X, ALU.max))
            done(v.tensor_tensor(low[:], upto[:], count[:], ALU.subtract))
            dve.wait_ge(p_rank, 1)
            v.tensor_copy(over[:, 0:1], ps_o[0:HI, 1, 0:1]).then_inc(p_upto, 1)
            dve.wait_ge(p_upto, 2)
            v.tensor_scalar(low[:], low[:], over[:, 0:1], None, ALU.add).then_inc(p_low, 1)
            dve.wait_ge(p_rank, 2)
            done(v.tensor_scalar(flag[:], ps_o[0:1, 1, 512:513], 1.0, None, ALU.min))
            dve.wait_ge(p_lowin, 16)
            done(v.tensor_scalar(row0[:], low_w[:], 1.0 / CAP, -(CAP // 2) / CAP, ALU.mult, ALU.add))
            done(v.tensor_scalar(row0f[:], row0[:], float(EROWS - 1), None, ALU.min))
            v.tensor_copy(row0[:], row0f[:])
            v.tensor_scalar(row1[:], row0f[:], 1.0, float(EROWS - 1), ALU.add, ALU.min).then_inc(p_rows, 1)
            done(v.scalar_tensor_tensor(out=start[:], in0=row0f[:], scalar=-float(CAP), in1=low_w[:],
                                        op0=ALU.mult, op1=ALU.add))
            for q in range(GROUPS):
                v.tensor_scalar(in0[:, q, :], iota_slot[:], start[:, q:q + 1], None, ALU.is_ge)
                v.tensor_scalar(in1[:, q, :], iota_slot[:], start[:, q:q + 1], None, ALU.is_lt)
            done(v.memset(dtab[:], 0.0))
            dve.wait_ge(p_fetch, 16 * 8 * GROUPS)
            for f in range(4):
                a = fetched_i[:, f] if f < 2 else fetched_f[:, f - 2]
                v.tensor_tensor(part[:, 0], a[:, 0], in0[:], ALU.mult)
                done(v.tensor_tensor(part[:, 1], a[:, 1], in1[:], ALU.mult))
                done(v.tensor_tensor(table[:, f], part[:, 0], part[:, 1], ALU.add))
                dve.sem_inc(p_tab, 1)
            to = params[:].bitcast(F32)
            wins = BATCHES * NW

            def column(tab, at):
                return tab[0:CAP, 0:BATCHES, at:at + NW]

            def windows(ap):
                return ap[0:CAP, 0:wins].rearrange("p (n k) -> p n k", k=NW)

            dve.wait_ge(p_tabt, 1)
            v.tensor_copy(column(params, SRC), windows(ps_t)).then_inc(p_tabc, 1)
            dve.wait_ge(p_tabt, 2)
            v.tensor_copy(column(params, DST), windows(ps_t))
            done(v.tensor_tensor(dtab[0:CAP, :], ps_t[0:CAP, 0:WINDOWS], win_base[0:CAP, :], ALU.subtract))
            dve.sem_inc(p_tabc, 1)
            done(v.tensor_scalar(inside[0:CAP, :], dtab[0:CAP, :], 0.0, None, ALU.is_ge))
            done(v.scalar_tensor_tensor(out=inside[0:CAP, :], in0=dtab[0:CAP, :], scalar=float(WIN),
                                        in1=inside[0:CAP, :], op0=ALU.is_lt, op1=ALU.mult))
            done(v.scalar_tensor_tensor(out=dtab[0:CAP, :], in0=dtab[0:CAP, :], scalar=-NOWHERE,
                                        in1=inside[0:CAP, :], op0=ALU.add, op1=ALU.mult))
            done(v.memset(to[:, :, LOC:LOC + NW], NOWHERE))
            v.tensor_scalar(column(to, LOC), windows(dtab), NOWHERE, None, ALU.add)
            dve.wait_ge(p_tabt, 3)
            v.tensor_copy(column(to, EWT), windows(ps_t)).then_inc(p_tabc, 1)
            dve.wait_ge(p_tabt, 4)
            done(v.tensor_copy(column(to, DEG), windows(ps_t)))

        def node_rows(l, b, r=NT):
            return nodes[l][bass.ds(BATCH * b.n, r * P), :].rearrange("(r p) c -> p r c", p=P)

        def edge_params(b, at, n=NW):
            return ep[:, b.slot, at:at + n].bitcast(F32)

        def sp_layer(sp, l):
            store = {0: 6, 1: 5, 2: 5, 3: 4}[l]
            width = P if l == 0 else ROW

            def body(t):
                b = t
                if b.real:
                    gathered.wait(sp, l, b.back(SLOTS))
                    e_sel.wait(sp, l, b.back(SLOTS))
                    if l in (1, 2):
                        e_scale.wait(sp, l, b.back(SLOTS))
                    sp.dma_start(ep[:, b.slot, :], params[:, bass.ds(b.n, 1), :].rearrange("p a c -> p (a c)")
                                 ).then_inc(ep_in.sems[b.slot], 16)
                    n_out.wait(sp, l, b.back(SLOTS))
                    if l:
                        n_norm.wait(sp, l, b.back(SLOTS))
                    if l == 0 and b.n is not None and isinstance(b.n, int) and b.n == BATCHES - 1:
                        sp.dma_start(xn[:, b.slot, 0, 0:P], x[NODES - TAIL:NODES - TAIL + P, :]
                                     ).then_inc(x_in.sems[b.slot], 16)
                        sp.dma_start(xn[0:TAIL - P, b.slot, 1, 0:P], x[NODES - TAIL + P:NODES, :]
                                     ).then_inc(x_tail, 16)
                    else:
                        sp.dma_start(xn[:, b.slot, :, 0:width], node_rows(l, b)).then_inc(x_in.sems[b.slot], 16)
                b = t.back(store)
                if not b.real:
                    return
                if l < 3:
                    n_fin.wait(sp, l, b)
                    sp.dma_start(node_rows(l + 1, b), xo[:, b.slot]).then_inc(x_stored.sems[b.slot], 16)
                else:
                    n_out.wait(sp, l, b)
                    if isinstance(b.n, int) and b.n == BATCHES - 1:
                        sp.dma_start(out[NODES - TAIL:NODES - TAIL + P, :], xo[:, b.slot, 0, 0:P]
                                     ).then_inc(x_stored.sems[b.slot], 16)
                        sp.dma_start(out[NODES - TAIL + P:NODES, :], xo[0:TAIL - P, b.slot, 1, 0:P]
                                     ).then_inc(out_tail, 16)
                        sp.wait_ge(out_tail, 16)
                    else:
                        sp.dma_start(out[bass.ds(BATCH * b.n, BATCH), :].rearrange("(r p) c -> p r c", p=P),
                                     xo[:, b.slot, :, 0:P]).then_inc(x_stored.sems[b.slot], 16)

            steps(sp, store, body)
            x_stored.all(sp, l)

        def pool_layer(pool, l):
            width = P if l == 0 else ROW

            def body(b):
                ep_in.wait(pool, l, b)
                e_norm.wait(pool, l, b.back(SLOTS))
                if l in (1, 2):
                    e_scale.wait(pool, l, b.back(SLOTS))
                if l == 3:
                    e_normd.wait(pool, l, b.back(SLOTS))
                settle(pool, moved)
                for k in range(2 * NW if l == 3 else NW):
                    nc.gpsimd.indirect_dma_start(
                        rows[:, b.slot, k, 0:width], None, nodes[l],
                        bass.IndirectOffsetOnAxis(ap=ep[:, b.slot, k:k + 1], axis=0)
                    ).then_inc(gathered.sems[b.slot], 16)

            steps(pool, 0, body)

        def new_row_stats(dve, l, b, mid):
            s = b.slot
            n_mm.wait(dve, l, b)
            x_in.wait(dve, l, b)
            if l == 0 and isinstance(b.n, int) and b.n == BATCHES - 1:
                dve.wait_ge(x_tail, 16)
            x_stored.wait(dve, l, b.back(SLOTS))
            if l == 0 or l == 2:
                nc.vector.tensor_tensor(xo[:, s, :, 0:P], update(l, b), xn[:, s, :, 0:P], ALU.add
                                        ).then_inc(n_out.sem, 1)
            else:
                nc.vector.scalar_tensor_tensor(out=xo[:, s, :, 0:P], in0=update(l, b), scalar=0.0,
                                               in1=xn[:, s, :, 0:P], op0=ALU.max, op1=ALU.add
                                               ).then_inc(n_out.sem, 1)
            mid(0)
            n_out.wait(dve, l, b)
            for r in range(NT):
                last = nc.vector.bn_stats(stat[:, s, r, :], xo[:, s, r, 0:P])
            last.then_inc(n_stats.sem, 1)
            mid(1)
            n_stats.wait(dve, l, b)
            n_std.wait(dve, l, b.back(SLOTS))
            settle(dve, moved)
            for r in range(NT):
                last = nc.vector.bn_aggr(var[:, s, r, :], stat[:, s, r, :])
            last.then_inc(n_aggr.sem, 1)
            mid(2)
            n_aggr.wait(dve, l, b)
            nc.vector.tensor_scalar(xo[:, s, :, NMEAN], var[:, s, :, 0], -1.0, None, ALU.mult
                                    ).then_inc(n_var.sem, 1)

        def update(l, b):
            return ps_o[:, 0 if l == 3 else b.c % 2, 0:BATCH].rearrange("p (r f) -> p r f", f=P)

        def finish_rows(dve, l, b):
            s = b.slot
            n_std.wait(dve, l, b)
            nc.vector.reciprocal(xo[:, s, :, INV], std[:, s, :]).then_inc(n_inv.sem, 1)
            n_inv.wait(dve, l, b)
            nc.vector.tensor_tensor(xo[:, s, :, NMI], xo[:, s, :, NMEAN], xo[:, s, :, INV], ALU.mult
                                    ).then_inc(n_fin.sem, 1)

        def dve_layer(dve, l):
            v = nc.vector

            def body0(t):
                b = t.back(6)
                if b.real:
                    finish_rows(dve, l, b)
                b = t.back(3)
                if b.real:
                    s = b.slot
                    e_std.wait(dve, l, b)
                    e_norm.wait(dve, l, b.back(SLOTS))
                    v.reciprocal(einv[:, s, :], estd[:, s, :]).then_inc(e_inv.sem, 1)
                    ep_in.wait(dve, l, b)
                    e_agg.wait(dve, l, b.back(SLOTS))
                    v.tensor_tensor(sel[:, s, 0:BATCH].rearrange("p (w j) -> p w j", w=NW), iota_win[:],
                                    edge_params(b, LOC).rearrange("p (w a) -> p w a", a=1)
                                    .to_broadcast([P, NW, WIN]), ALU.is_equal).then_inc(e_sel.sem, 1)
                    e_inv.wait(dve, l, b)
                    v.scalar_tensor_tensor(out=enmi[:, s, :], in0=evar[:, s, :, 0], scalar=-1.0,
                                           in1=einv[:, s, :], op0=ALU.mult, op1=ALU.mult).then_inc(e_nmi.sem, 1)
                e = t.back(2)

                def mid(k):
                    if not e.real:
                        return
                    s = e.slot
                    if k == 0:
                        gathered.wait(dve, l, e)
                        for w in range(NW):
                            last = v.bn_stats(estat[:, s, w, :], rows[:, s, w, 0:P])
                        last.then_inc(e_stats.sem, 1)
                    if k == 1:
                        e_stats.wait(dve, l, e)
                        e_nmi.wait(dve, l, e.back(SLOTS))
                        e_std.wait(dve, l, e.back(SLOTS))
                        settle(dve, moved)
                        for w in range(NW):
                            last = v.bn_aggr(evar[:, s, w, :], estat[:, s, w, :])
                        last.then_inc(e_var.sem, 1)

                b = t.back(5)
                if b.real:
                    new_row_stats(dve, l, b, mid)
                else:
                    mid(0)
                    mid(1)

            def body12(t):
                b = t.back(5)
                if b.real:
                    finish_rows(dve, l, b)
                b = t.back(3)
                if l == 2 and b.real:
                    s = b.slot
                    n_tr.wait(dve, l, b)
                    n_aggt.wait(dve, l, b)
                    n_mm.wait(dve, l, b.back(SLOTS))
                    v.scalar_tensor_tensor(out=prod_t[:, s, :], in0=ps_t[:, 0:BATCH], scalar=0.0,
                                           in1=agg_t[:, s, :], op0=ALU.max, op1=ALU.mult).then_inc(n_prod.sem, 1)
                e = t.back(2)

                def mid(k):
                    if k or not e.real:
                        return
                    s = e.slot
                    gathered.wait(dve, l, e)
                    ep_in.wait(dve, l, e)
                    v.tensor_tensor(scale[:, s, :], rows[:, s, 0:NW, INV], edge_params(e, DEG if l == 1 else EWT),
                                    ALU.mult).then_inc(e_scale.sem, 1)
                    e_agg.wait(dve, l, e.back(SLOTS))
                    for w in range(NW):
                        last = v.tensor_scalar(msg[:, s, w, :], rows[:, s, w, 0:P], rows[:, s, w, NMEAN:NMEAN + 1],
                                               0.0, ALU.add, ALU.max)
                    last.then_inc(e_norm.sem, 1)
                    e_scale.wait(dve, l, e)
                    for w in range(NW):
                        last = v.tensor_scalar(sel[:, s, WIN * w:WIN * (w + 1)], iota_win[:, 0, :],
                                               edge_params(e, LOC + w, 1), scale[:, s, w:w + 1],
                                               ALU.is_equal, ALU.mult)
                    last.then_inc(e_sel.sem, 1)

                mid(0)
                b = t.back(4)
                if b.real:
                    new_row_stats(dve, l, b, lambda k: None)

            def body3(t):
                b = t.back(3)
                if b.real:
                    s = b.slot
                    e_eta.wait(dve, l, b)
                    n_mm.wait(dve, l, b.back(SLOTS))
                    v.tensor_tensor(msg[:, s], ps_o[:, 1, :].rearrange("p (w c) -> p w c", w=NW)[:, :, P:2 * P],
                                    eta[:, b.c % 2], ALU.mult).then_inc(e_msg.sem, 1)
                e = t.back(2)
                if e.real:
                    s = e.slot
                    gathered.wait(dve, l, e)
                    e_tr.wait(dve, l, e.back(SLOTS))
                    for w in range(NW):
                        last = v.tensor_scalar(eh[:, s, w, :], rows[:, s, w, 0:P], rows[:, s, w, INV:INV + 1],
                                               rows[:, s, w, NMI:NMI + 1], ALU.mult, ALU.add)
                    last.then_inc(e_norm.sem, 1)
                    ep_in.wait(dve, l, e)
                    n_mm.wait(dve, l, e.back(SLOTS))
                    for w in range(NW):
                        last = v.tensor_scalar(sel[:, s, 2 * P * w:2 * P * (w + 1)], iota_pair[:, w, :],
                                               edge_params(e, LOC + w, 1), None, ALU.is_equal)
                    last.then_inc(e_sel.sem, 1)
                b = t.back(4)
                if b.real:
                    s = b.slot
                    n_mm.wait(dve, l, b)
                    x_in.wait(dve, l, b)
                    x_stored.wait(dve, l, b.back(SLOTS))
                    v.tensor_tensor(xo[:, s, :, 0:P], update(l, b), xn[:, s, :, 0:P], ALU.add
                                    ).then_inc(n_out.sem, 1)

            steps(dve, (6, 5, 5, 4)[l], (body0, body12, body12, body3)[l])

        def act_layer(act, l):
            a = nc.scalar

            def new_std(b):
                n_var.wait(act, l, b)
                n_fin.wait(act, l, b.back(SLOTS))
                a.activation(std[:, b.slot, :], var[:, b.slot, :, 1], ACT.Sqrt, bias=eps_col[:]
                             ).then_inc(n_std.sem, 1)

            def normalise_nodes(b):
                s = b.slot
                x_in.wait(act, l, b)
                n_tr.wait(act, l, b.back(SLOTS))
                for r in range(NT):
                    last = a.activation(xh[:, s, r, :], xn[:, s, r, 0:P], ACT.Identity,
                                        bias=xn[:, s, r, NMI:NMI + 1], scale=xn[:, s, r, INV:INV + 1])
                last.then_inc(n_norm.sem, 1)

            def take_aggregate(b):
                s = b.slot
                e_agg.wait(act, l, b)
                n_mm.wait(act, l, b.back(SLOTS))
                a.copy(agg_t[:, s, :].rearrange("p (w j) -> p w j", w=NW),
                       ps_e[:].rearrange("p (w j) -> p w j", w=NW)[:, :, 0:WIN]).then_inc(n_aggt.sem, 1)

            def take_nodes(b):
                s = b.slot
                n_tr.wait(act, l, b)
                n_mm.wait(act, l, b.back(SLOTS))
                a.activation(h_t[:, s, :], ps_t[:, 0:BATCH], ACT.Relu).then_inc(n_ht.sem, 1)

            def body0(t):
                b = t.back(3)
                if b.real:
                    s = b.slot
                    e_nmi.wait(act, l, b)
                    gathered.wait(act, l, b)
                    e_agg.wait(act, l, b.back(SLOTS))
                    for w in range(NW):
                        last = a.activation(msg[:, s, w, :], rows[:, s, w, 0:P], ACT.Relu,
                                            bias=enmi[:, s, w:w + 1], scale=einv[:, s, w:w + 1])
                    last.then_inc(e_norm.sem, 1)
                    take_aggregate(b)
                b = t.back(2)
                if b.real:
                    e_var.wait(act, l, b)
                    e_inv.wait(act, l, b.back(SLOTS))
                    a.activation(estd[:, b.slot, :], evar[:, b.slot, :, 1], ACT.Sqrt, bias=eps_col[:]
                                 ).then_inc(e_std.sem, 1)
                b = t.back(5)
                if b.real:
                    new_std(b)

            def body12(t):
                b = t.back(2)
                if b.real:
                    normalise_nodes(b)
                    take_aggregate(b)
                    if l == 1:
                        take_nodes(b)
                b = t.back(4)
                if b.real:
                    new_std(b)

            def body3(t):
                b = t.back(3)
                if b.real:
                    e_gate.wait(act, l, b)
                    e_msg.wait(act, l, b.back(2))
                    a.activation(eta[:, b.c % 2], ps_o[:, 1, :].rearrange("p (w c) -> p w c", w=NW)[:, :, 0:P],
                                 ACT.Sigmoid).then_inc(e_eta.sem, 1)
                b = t.back(2)
                if b.real:
                    s = b.slot
                    gathered.wait(act, l, b)
                    e_tr.wait(act, l, b.back(SLOTS))
                    for w in range(NW, 2 * NW):
                        last = a.activation(eh[:, s, w, :], rows[:, s, w, 0:P], ACT.Identity,
                                            bias=rows[:, s, w, NMI:NMI + 1], scale=rows[:, s, w, INV:INV + 1])
                    last.then_inc(e_normd.sem, 1)
                    normalise_nodes(b)
                    e_tr.wait(act, l, b)
                    e_gate.wait(act, l, b.back(2))
                    a.activation(eh_t[:, b.c % 2], ps_e[:].rearrange("p (w c) -> p w c", c=P), ACT.Relu
                                 ).then_inc(e_ht.sem, 1)
                    take_nodes(b)

            steps(act, (5, 4, 4, 3)[l], (body0, body12, body12, body3)[l])

        def pe_layer(pe, l):
            def aggregate(b):
                s = b.slot
                e_norm.wait(pe, l, b)
                e_sel.wait(pe, l, b)
                n_aggt.wait(pe, l, b.back(1))
                for w in range(NW):
                    mm = pe.matmul(ps_e[:, 2 * P * w:2 * P * w + WIN], msg[:, s, w, :],
                                   sel[:, s, WIN * w:WIN * (w + 1)], start=True, stop=True)
                mm.then_inc(e_agg.sem, 1)

            def turn_nodes(b):
                n_norm.wait(pe, l, b)
                (n_prod if l == 2 else n_ht).wait(pe, l, b.back(1))
                for r in range(NT):
                    mm = pe.transpose(ps_t[:, P * r:P * (r + 1)], xh[:, b.slot, r, :], ident[:])
                mm.then_inc(n_tr.sem, 1)

            def start_with(b, bias):
                o = 0 if l == 3 else b.c % 2
                pe.matmul(ps_o[:, o, 0:4 * P], ones3[:], bias[:].rearrange("p q f -> p (q f)"),
                          start=True, stop=False, skip_group_check=True)
                pe.matmul(ps_o[:, o, 4 * P:BATCH], ones3[:], bias[:, 0, :],
                          start=True, stop=False, skip_group_check=True)

            def body012(t):
                b = t.back(3 if l == 0 else 2)
                if b.real:
                    aggregate(b)
                    if l:
                        turn_nodes(b)
                b = t.back(4 if l == 0 else 3)
                if not b.real:
                    return
                s = b.slot
                n_aggt.wait(pe, l, b)
                if l == 1:
                    n_ht.wait(pe, l, b)
                if l == 2:
                    n_prod.wait(pe, l, b)
                n_out.wait(pe, l, b.back(2))
                if l < 2:
                    start_with(b, (bias0, bias1)[l])
                terms = {0: [(agg_t, w0t)], 1: [(h_t, wselft), (agg_t, wneit)], 2: [(agg_t, w1), (prod_t, w2)]}[l]
                for r in range(NT):
                    for k, (left, w) in enumerate(terms):
                        mm = pe.matmul(ps_o[:, b.c % 2, P * r:P * (r + 1)], left[:, s, P * r:P * (r + 1)], w[:],
                                       start=(l == 2 and k == 0), stop=(k == len(terms) - 1),
                                       skip_group_check=True)
                mm.then_inc(n_mm.sem, 1)

            def body3(t):
                e = t.back(2)
                if e.real:
                    s = e.slot
                    e_norm.wait(pe, l, e)
                    e_normd.wait(pe, l, e)
                    e_ht.wait(pe, l, e.back(1))
                    for w in range(2 * NW):
                        mm = pe.transpose(ps_e[:, P * w:P * (w + 1)], eh[:, s, w, :], ident[:])
                    mm.then_inc(e_tr.sem, 1)
                b = t.back(3)
                if b.real:
                    s = b.slot
                    n_out.wait(pe, l, b.back(1))
                    n_ht.wait(pe, l, b)
                    start_with(b, bias3)
                    for r in range(NT):
                        pe.matmul(ps_o[:, 0, P * r:P * (r + 1)], h_t[:, s, P * r:P * (r + 1)], wr[:],
                                  start=False, stop=False, skip_group_check=True)
                    e_sel.wait(pe, l, b)
                    e_msg.wait(pe, l, b)
                    for w in range(NW):
                        for k in range(2):
                            mm = pe.matmul(ps_o[:, 0, P * (w + k):P * (w + k + 1)],
                                           sel[:, s, P * (2 * w + k):P * (2 * w + k + 1)], msg[:, s, w, :],
                                           start=False, stop=(k == 0 or w == NW - 1), skip_group_check=True)
                    mm.then_inc(n_mm.sem, 1)
                if e.real:
                    turn_nodes(e)
                    e_ht.wait(pe, l, e)
                    e_msg.wait(pe, l, e.back(1))
                    for w in range(0, NW, 2):
                        pe.matmul(ps_o[:, 1, 2 * P * w:2 * P * (w + 2)], ones3[:],
                                  biase[:].rearrange("p q f -> p (q f)"), start=True, stop=False,
                                  skip_group_check=True)
                    for w in range(NW):
                        pe.matmul(ps_o[:, 1, 2 * P * w:2 * P * (w + 1)], eh_t[:, e.c % 2, w, :], wg_ws[:],
                                  start=False, stop=False, skip_group_check=True)
                        mm = pe.matmul(ps_o[:, 1, 2 * P * w:2 * P * w + P], eh_t[:, e.c % 2, NW + w, :], wg_rec[:],
                                       start=False, stop=True, skip_group_check=True)
                    mm.then_inc(e_gate.sem, 1)

            steps(pe, (4, 3, 3, 3)[l], body3 if l == 3 else body012)

        key_of = {0: 1, 1: 1, 2: 0, 3: 1}
        fetch = {0: (0,), 1: (0,), 2: (1,), 3: (0, 1)}

        def fetches(l, k):
            return 16 * TILES * sum(len(fetch[m]) for m in range(l - k, l)), 16 * len(fetch[l])

        class Steps:

            def __init__(self, eng, sem, base, per):
                self.eng, self.sem, self.base, self.per = eng, sem, base, per

            def turn(self, t):
                self.at, self.n = self.base + self.per * t, 0

            def __call__(self, ins):
                self.n += 1
                assert self.n <= self.per
                ins.then_inc(self.sem, 1)
                self.eng.wait_ge(self.sem, self.at + self.n)

        EDGE_STEPS = 13
        NODE_STEPS = 11

        def general_zero(eng, k):
            with eng.Fori(0, BATCHES) as t:
                eng.dma_start(sums[bass.ds(BATCH * t, BATCH), :].rearrange("(r p) c -> p r c", p=P),
                              g_zero[:].rearrange("p (r c) -> p r c", c=SUM)).then_inc(g_zeroed, 16)
            eng.dma_start(sums[TRASH:TRASH + P, :], g_zero[:, 0:SUM]).then_inc(g_zeroed, 16)
            eng.wait_ge(g_zeroed, 16 * (BATCHES + 1) * (k + 1))

        def sp_edges(sp, l, k):
            general_zero(sp, k)
            with sp.Fori(0, TILES) as t:
                sp.dma_start(g_edge[:], edges[:, bass.ds(t, 1), :].rearrange("p a c -> p (a c)")
                             ).then_inc(g_edge_in, 16)
                sp.wait_ge(g_added, 16 * TILES * k + 16 * t + 16)
                settle(sp, moved)

        def pool_edges(pool, l, k):
            fetched, own = fetches(l, k)
            pool.wait_ge(g_zeroed, 16 * (BATCHES + 1) * (k + 1))
            with pool.Fori(0, TILES) as t:
                pool.wait_ge(g_edge_in, 16 * TILES * k + 16 * t + 16)
                settle(pool, moved)
                for j, f in enumerate(fetch[l]):
                    nc.gpsimd.indirect_dma_start(
                        rows[0:CAP, 0, j, 0:P], None, nodes[l],
                        bass.IndirectOffsetOnAxis(ap=g_edge[:, f:f + 1], axis=0)).then_inc(g_rows_in, 16)
                pool.wait_ge(g_totald, TILES * k + t + 1)
                settle(pool, moved)
                nc.gpsimd.indirect_dma_start(
                    sums, bass.IndirectOffsetOnAxis(ap=g_to[:, 0:1], axis=0), g_total[:], None,
                    compute_op=ALU.add).then_inc(g_added, 16)
            pool.wait_ge(g_added, 16 * TILES * (k + 1))

        def dve_edges(dve, l, k):
            v = nc.vector
            then = Steps(dve, g_step, TILES * EDGE_STEPS * k, EDGE_STEPS)
            fetched, own = fetches(l, k)
            with dve.Fori(0, TILES) as t:
                then.turn(t)
                n = TILES * k + t + 1
                dve.wait_ge(g_edge_in, 16 * TILES * k + 16 * t + 16)
                then(v.tensor_copy(g_key[:], g_edge[:, key_of[l]:key_of[l] + 1]))
                v.tensor_scalar(g_diag[:], ident[0:CAP, 0:CAP], g_key[:], None, ALU.mult).then_inc(g_diagd, 1)
                dve.wait_ge(g_keys, n)
                then(v.tensor_scalar(g_same[:], ps_e[0:CAP, 0:CAP], g_key[:], None, ALU.is_equal))
                then(v.tensor_tensor(g_before[:], g_same[:], g_earlier[:], ALU.mult))
                then(v.tensor_reduce(g_prior[:], g_before[:], AX.X, ALU.max))
                then(v.tensor_tensor(g_tof[:], g_trash[:], g_key[:], ALU.subtract))
                then(v.scalar_tensor_tensor(out=g_tof[:], in0=g_tof[:], scalar=g_prior[:], in1=g_key[:],
                                            op0=ALU.mult, op1=ALU.add))
                then(v.tensor_copy(g_to[:], g_tof[:]))
                m = len(fetch[l])
                dve.wait_ge(g_rows_in, fetched + own * t + own)
                for j in range(m):
                    last = v.bn_stats(estat[0:CAP, 0, j, :], rows[0:CAP, 0, j, 0:P])
                then(last)
                settle(dve, moved)
                for j in range(m):
                    last = v.bn_aggr(evar[0:CAP, 0, j, :], estat[0:CAP, 0, j, :])
                last.then_inc(g_var, 1)
                dve.wait_ge(g_std, n)
                then(v.reciprocal(einv[0:CAP, 0, 0:m], estd[0:CAP, 0, 0:m]))
                then(v.scalar_tensor_tensor(out=enmi[0:CAP, 0, 0:m], in0=evar[0:CAP, 0, 0:m, 0], scalar=-1.0,
                                            in1=einv[0:CAP, 0, 0:m], op0=ALU.mult, op1=ALU.mult))
                for j in range(m):
                    last = v.tensor_scalar(eh[0:CAP, 0, j, :], rows[0:CAP, 0, j, 0:P], einv[0:CAP, 0, j:j + 1],
                                           enmi[0:CAP, 0, j:j + 1], ALU.mult, ALU.add)
                if l == 3:
                    last.then_inc(g_hd, 1)
                    dve.wait_ge(g_eta, t + 1)
                    v.tensor_tensor(g_msg[:, 0:P], ps_o[0:CAP, 1, P:2 * P], eta[0:CAP, 0, 0, :], ALU.mult
                                    ).then_inc(g_msgd, 1)
                else:
                    then(last)
                    w = g_edge[:, 2:3].bitcast(F32) if l == 2 else 1.0
                    v.tensor_scalar(g_msg[:, 0:P], eh[0:CAP, 0, 0, :], 0.0, w, ALU.max, ALU.mult
                                    ).then_inc(g_msgd, 1)
                dve.wait_ge(g_comb, n)
                v.tensor_copy(g_total[:], ps_e[0:CAP, 512:512 + SUM]).then_inc(g_totald, 1)
                while then.n < EDGE_STEPS:
                    then(v.memset(g_before[0:1, 0:1], 0.0))

        def act_edges(act, l, k):
            a = nc.scalar
            with act.Fori(0, TILES) as t:
                n = TILES * k + t + 1
                m = len(fetch[l])
                act.wait_ge(g_var, n)
                a.activation(estd[0:CAP, 0, 0:m], evar[0:CAP, 0, 0:m, 1], ACT.Sqrt, bias=eps_col[0:CAP, :]
                             ).then_inc(g_std, 1)
                if l == 3:
                    act.wait_ge(g_tr, t + 1)
                    a.activation(eh_t[:, 0, 0:2, 0:CAP], ps_t[:, 0:2 * P].rearrange("p (w c) -> p w c", c=P)[:, :, 0:CAP],
                                 ACT.Relu).then_inc(g_ht, 1)
                    act.wait_ge(g_gate, t + 1)
                    a.activation(eta[0:CAP, 0, 0, :], ps_o[0:CAP, 1, 0:P], ACT.Sigmoid).then_inc(g_eta, 1)

        def pe_edges(pe, l, k):
            with pe.Fori(0, TILES) as t:
                n = TILES * k + t + 1
                pe.wait_ge(g_diagd, n)
                pe.matmul(ps_e[0:CAP, 0:CAP], g_ones[:], g_diag[:], start=True, stop=True).then_inc(g_keys, 1)
                if l == 3:
                    pe.wait_ge(g_hd, t + 1)
                    for j in range(2):
                        mm = pe.transpose(ps_t[:, P * j:P * j + CAP], eh[0:CAP, 0, j, :], ident[0:CAP, 0:CAP])
                    mm.then_inc(g_tr, 1)
                    pe.wait_ge(g_ht, t + 1)
                    pe.matmul(ps_o[0:CAP, 1, 0:2 * P], ones3[:, 0:CAP], biase[:, 0:2, :].rearrange("p q f -> p (q f)"),
                              start=True, stop=False, skip_group_check=True)
                    pe.matmul(ps_o[0:CAP, 1, 0:2 * P], eh_t[:, 0, 0, 0:CAP], wg_ws[:],
                              start=False, stop=False, skip_group_check=True)
                    pe.matmul(ps_o[0:CAP, 1, 0:P], eh_t[:, 0, 1, 0:CAP], wg_rec[:],
                              start=False, stop=True, skip_group_check=True).then_inc(g_gate, 1)
                pe.wait_ge(g_msgd, n)
                pe.matmul(ps_e[0:CAP, 512:512 + SUM], g_same[:], g_msg[:], start=True, stop=True).then_inc(g_comb, 1)

        def per_batch(eng, body):
            with eng.Fori(0, BATCHES - 1) as t:
                body(t)
            body(BATCHES - 1)

        def sp_nodes(sp, l, k):
            def body(t):
                n = BATCHES * k + t
                last = isinstance(t, int)
                at = Batch(0, 0)
                at.n = t
                if l == 0 and last:
                    sp.dma_start(xn[:, 0, 0, 0:P], x[NODES - TAIL:NODES - TAIL + P, :]).then_inc(gn_in, 16)
                    sp.wait_ge(gn_in, 16 * n + 16)
                    sp.dma_start(xn[0:TAIL - P, 0, 1, 0:P], x[NODES - TAIL + P:NODES, :]).then_inc(x_tail, 16)
                else:
                    sp.dma_start(xn[:, 0, :, 0:P], node_rows(l, at)[:, :, 0:P]).then_inc(gn_in, 16)
                sp.dma_start(g_sums[:], sums[bass.ds(BATCH * t, BATCH), :].rearrange("(r p) c -> p r c", p=P)
                             ).then_inc(gn_sums_in, 16)
                sp.wait_ge(gn_out, n + 1)
                settle(sp, moved)
                if l < 3:
                    sp.dma_start(node_rows(l + 1, at), xo[:, 0]).then_inc(gn_stored, 16)
                elif last:
                    sp.dma_start(out[NODES - TAIL:NODES - TAIL + P, :], xo[:, 0, 0, 0:P]).then_inc(gn_stored, 16)
                    sp.dma_start(out[NODES - TAIL + P:NODES, :], xo[0:TAIL - P, 0, 1, 0:P]).then_inc(out_tail, 16)
                    sp.wait_ge(out_tail, 16)
                else:
                    sp.dma_start(out[bass.ds(BATCH * t, BATCH), :].rearrange("(r p) c -> p r c", p=P),
                                 xo[:, 0, :, 0:P]).then_inc(gn_stored, 16)
                sp.wait_ge(gn_stored, 16 * n + 16)
                settle(sp, moved)

            per_batch(sp, body)

        def dve_nodes(dve, l, k):
            v = nc.vector
            then = Steps(dve, gn_step, BATCHES * NODE_STEPS * k, NODE_STEPS)
            stats_of = {0: xn, 1: xo}

            def body(t):
                then.turn(t)
                n = BATCHES * k + t + 1
                dve.wait_ge(gn_in, 16 * n)
                if l == 0 and isinstance(t, int):
                    dve.wait_ge(x_tail, 16)
                for again, x_rows in enumerate((xn, xo)):
                    for r in range(NT):
                        last = v.bn_stats(stat[:, 0, r, :], x_rows[:, 0, r, 0:P])
                    then(last)
                    settle(dve, moved)
                    for r in range(NT):
                        last = v.bn_aggr(var[:, 0, r, :], stat[:, 0, r, :])
                    last.then_inc(gn_var, 1)
                    dve.wait_ge(gn_std, 2 * n - 1 + again)
                    then(v.reciprocal(x_rows[:, 0, :, INV], std[:, 0, :]))
                    then(v.tensor_scalar(x_rows[:, 0, :, NMEAN], var[:, 0, :, 0], -1.0, None, ALU.mult))
                    last = v.tensor_tensor(x_rows[:, 0, :, NMI], x_rows[:, 0, :, NMEAN], x_rows[:, 0, :, INV], ALU.mult)
                    if again:
                        last.then_inc(gn_out, 1)
                        break
                    then(last)
                    for r in range(NT):
                        last = v.tensor_scalar(xh[:, 0, r, :], xn[:, 0, r, 0:P], xn[:, 0, r, INV:INV + 1],
                                               xn[:, 0, r, NMI:NMI + 1], ALU.mult, ALU.add)
                    dve.wait_ge(gn_sums_in, 16 * n)
                    if l == 1:
                        then(v.tensor_scalar(g_deg[:], g_sums[:, :, P], 1.0, None, ALU.max))
                        then(v.reciprocal(g_deg[:], g_deg[:]))
                        for r in range(NT):
                            last = v.tensor_scalar(g_mean[:, r, :], g_sums[:, r, 0:P], g_deg[:, r:r + 1], None, ALU.mult)
                    else:
                        last = v.tensor_copy(g_mean[:], g_sums[:, :, 0:P])
                    last.then_inc(gn_ready, 1)
                    if l == 2:
                        dve.wait_ge(gn_take, n)
                        v.tensor_tensor(prod_t[:, 0, :], agg_t[:, 0, :], h_t[:, 0, :], ALU.mult).then_inc(gn_prod, 1)
                    dve.wait_ge(gn_mm, n)
                    add_to = xn[:, 0, :, 0:P]
                    if l == 3:
                        then(v.tensor_tensor(g_mean[:], g_mean[:], xn[:, 0, :, 0:P], ALU.add))
                        add_to = g_mean[:]
                    new = ps_o[:, 0, 0:BATCH].rearrange("p (r f) -> p r f", f=P)
                    if l == 1:
                        then(v.scalar_tensor_tensor(out=xo[:, 0, :, 0:P], in0=new, scalar=0.0, in1=add_to,
                                                    op0=ALU.max, op1=ALU.add))
                    else:
                        then(v.tensor_tensor(xo[:, 0, :, 0:P], new, add_to, ALU.add))
                while then.n < NODE_STEPS:
                    then(v.memset(g_deg[0:1, 0:1], 0.0))

            per_batch(dve, body)

        def act_nodes(act, l, k):
            a = nc.scalar

            def body(t):
                n = BATCHES * k + t + 1
                act.wait_ge(gn_var, 2 * n - 1)
                a.activation(std[:, 0, :], var[:, 0, :, 1], ACT.Sqrt, bias=eps_col[:]).then_inc(gn_std, 1)
                act.wait_ge(gn_tr, n)
                a.copy(agg_t[:, 0, :], ps_e[:, 0:BATCH])
                a.activation(h_t[:, 0, :], ps_t[:, 0:BATCH], ACT.Relu).then_inc(gn_take, 1)
                act.wait_ge(gn_var, 2 * n)
                a.activation(std[:, 0, :], var[:, 0, :, 1], ACT.Sqrt, bias=eps_col[:]).then_inc(gn_std, 1)

            per_batch(act, body)

        def pe_nodes(pe, l, k):
            def body(t):
                n = BATCHES * k + t + 1
                pe.wait_ge(gn_ready, n)
                for r in range(NT):
                    pe.transpose(ps_e[:, P * r:P * (r + 1)], g_mean[:, r, :], ident[:])
                for r in range(NT):
                    mm = pe.transpose(ps_t[:, P * r:P * (r + 1)], xh[:, 0, r, :], ident[:])
                mm.then_inc(gn_tr, 1)
                pe.wait_ge(gn_take, n)
                bias = (bias0, bias1, None, bias3)[l]
                if l == 2:
                    pe.wait_ge(gn_prod, t + 1)
                else:
                    pe.matmul(ps_o[:, 0, 0:4 * P], ones3[:], bias[:].rearrange("p q f -> p (q f)"),
                              start=True, stop=False, skip_group_check=True)
                    pe.matmul(ps_o[:, 0, 4 * P:BATCH], ones3[:], bias[:, 0, :],
                              start=True, stop=False, skip_group_check=True)
                terms = {0: [(agg_t, w0t)], 1: [(h_t, wselft), (agg_t, wneit)], 2: [(agg_t, w1), (prod_t, w2)],
                         3: [(h_t, wr)]}[l]
                for r in range(NT):
                    for j, (left, w) in enumerate(terms):
                        mm = pe.matmul(ps_o[:, 0, P * r:P * (r + 1)], left[:, 0, P * r:P * (r + 1)], w[:],
                                       start=(l == 2 and j == 0), stop=(j == len(terms) - 1), skip_group_check=True)
                mm.then_inc(gn_mm, 1)

            per_batch(pe, body)

        block = ctx.enter_context(nc.Block())

        def program(eng, prepare, layer, edges_pass, nodes_pass):
            prepare(eng)
            join(eng, 1)
            general = eng.value_load(flag[0:1, 0:1], min_val=0, max_val=1)
            with eng.If(general > 0):
                for l in range(4):
                    edges_pass(eng, l, l)
                    join(eng, 2 + 2 * l)
                    nodes_pass(eng, l, l)
                    join(eng, 3 + 2 * l)
            with eng.Else():
                k = 1
                for l in range(4):
                    if l == 2:
                        edges_pass(eng, l, 0)
                        k += 1
                        join(eng, k)
                        nodes_pass(eng, l, 0)
                    else:
                        layer(eng, l)
                    k += 1
                    join(eng, k)

        def nothing(eng, l, k):
            pass

        @block.sync
        def _(sp):
            program(sp, sp_prepare, sp_layer, sp_edges, sp_nodes)

        @block.gpsimd
        def _(pool):
            program(pool, pool_prepare, pool_layer, pool_edges, nothing)

        @block.scalar
        def _(act):
            program(act, act_prepare, act_layer, act_edges, act_nodes)

        @block.tensor
        def _(pe):
            program(pe, pe_prepare, pe_layer, pe_edges, pe_nodes)

        @block.vector
        def _(dve):
            program(dve, dve_prepare, dve_layer, dve_edges, dve_nodes)


_INS = ["x", "src", "dst", "edge_weight", "L0_gnn_W", "L0_gnn_b", "L1_gnn_W_self", "L1_gnn_b_self",
        "L1_gnn_W_nei", "L1_gnn_b_nei", "L2_gnn_W1", "L2_gnn_W2", "L3_gnn_Wg", "L3_gnn_bg", "L3_gnn_Ws",
        "L3_gnn_bs", "L3_gnn_Wr", "L3_gnn_br"]


def kernel(**inputs):
    import concourse.bacc as bacc
    from concourse.bass_utils import run_bass_kernel_spmd

    nc = bacc.Bacc("TRN2", target_bir_lowering=False, num_devices=1)
    arrays, args = {}, []
    for name in _INS:
        a = np.ascontiguousarray(inputs[name])
        arrays[f"in_{name}"] = a
        args.append(nc.dram_tensor(f"in_{name}", a.shape, mybir.dt.from_np(a.dtype), kind="ExternalInput").ap())
    args.append(nc.dram_tensor("out_x", (NODES, P), F32, kind="ExternalOutput").ap())
    build(nc, *args)
    r = run_bass_kernel_spmd(nc, [arrays], core_ids=[0])
    return r.results[0]["out_x"]
```

```python
from contextlib import ExitStack

import numpy as np

import concourse.bass as bass
from concourse import mybir

F32 = mybir.dt.float32
BF16 = mybir.dt.bfloat16
F16 = mybir.dt.float16
I32 = mybir.dt.int32
ALU = mybir.AluOpType
ACT = mybir.ActivationFunctionType
AX = mybir.AxisListType

P = 128
NODES = 100000
EDGES = 50000
EPS = 1e-5
WIN = 160
NW = 4
BATCH = WIN * NW
NT = BATCH // P
BATCHES = -(-NODES // BATCH)
PADDED = BATCHES * BATCH
TAIL = NODES - (BATCHES - 1) * BATCH
CAP = 125
EROWS = EDGES // CAP
COLS = 400
HALO = CAP
SPAN = COLS + 2 * HALO
WINDOWS = 640
GROUPS = WINDOWS // P
HI = WINDOWS // 32
WUSED = BATCHES * NW
GROUP = 4
LAST_RANK = P
SLOTS = 4
ROW = P + 3
INV, NMEAN, NMI = P, P + 1, P + 2
PARAMS = 20
SRC, DST, LOC, DEG, EWT = 0, 4, 8, 12, 16
TILES = EDGES // CAP
TRASH = PADDED
SUM = P + 1
REC = 4
X_LATER = (2, 1, 1, 1)
STORE = (8, 7, 7, 5)
DVE_MSG = {1: 2, 2: 0}
NOWHERE = -4096.0


def settle(eng, moved):
    eng.sem_inc(moved, 1)


class Batch:

    def __init__(self, i, c):
        self.i, self.c = i, c
        self.n = SLOTS * i + c
        self.slot = c % SLOTS
        self.lap = i + c // SLOTS

    def back(self, k):
        return Batch(self.i, self.c - k)

    @property
    def before(self):
        return isinstance(self.n, int) and self.n < 0

    @property
    def real(self):
        return not isinstance(self.n, int) or 0 <= self.n < BATCHES


class Event:

    def __init__(self, sem, layers, moved):
        self.sem, self.layers, self.moved = sem, layers, moved

    def wait(self, eng, layer, b):
        if not b.before:
            base = BATCHES * sum(l < layer for l in self.layers)
            eng.wait_ge(self.sem, base + b.n + 1)
            if eng.engine == mybir.EngineType.SP and not isinstance(b.n, int):
                settle(eng, self.moved)


class Landed:

    def __init__(self, sems, per, moved):
        self.sems, self.per, self.moved = sems, per, moved

    def wait(self, eng, layer, b):
        if not b.before:
            laps = len(range(b.slot, BATCHES, SLOTS))
            base = sum(v for l, v in self.per.items() if l < layer) * laps
            eng.wait_ge(self.sems[b.slot], base + self.per[layer] * (b.lap + 1))
            if eng.engine == mybir.EngineType.SP and not isinstance(b.n, int):
                settle(eng, self.moved)

    def all(self, eng, layer):
        for s in range(SLOTS):
            last = Batch(0, range(s, BATCHES, SLOTS)[-1])
            last.slot, last.lap = s, last.n // SLOTS
            self.wait(eng, layer, last)


def steps(eng, depth, body):
    first = -(-depth // SLOTS) + 1
    last = (BATCHES - 1) // SLOTS
    for i in range(first):
        for u in range(SLOTS):
            body(Batch(i, u))
    with eng.Fori(first, last) as i:
        for u in range(SLOTS):
            body(Batch(i, u))
    for t in range(last * SLOTS, BATCHES + depth):
        body(Batch(t // SLOTS, t % SLOTS))


def build(nc, x, src, dst, edge_weight, W0, b0, W_self, b_self, W_nei, b_nei, W1, W2,
          Wg, bg, Ws, bs, Wr, br, out):
    ctx = ExitStack()
    early = ExitStack()
    with ctx:
        def sem(name):
            return ctx.enter_context(nc.semaphore(name))

        def sb(name, shape, dt=F32, of=ctx):
            return of.enter_context(nc.sbuf_tensor(name, shape, dt))

        def dram(name, shape, dt=F32):
            return nc.dram_tensor(name, shape, dt, kind="Internal").ap()

        nodes = [x, dram("x1", [PADDED, ROW]), dram("x2", [PADDED, ROW]), dram("x3", [PADDED, ROW])]
        sums = dram("sums", [PADDED + P, SUM])
        inv_dram = dram("inv_dram", [EDGES])
        low_dram = dram("low_dram", [WINDOWS])
        by_src = dram("by_src", [LAST_RANK * WINDOWS + EDGES, REC], I32)

        ident = sb("ident", [P, P])
        iota_win = sb("iota_win", [P, NW, WIN])
        iota_pair = sb("iota_pair", [P, NW, 2 * P])
        params = sb("params", [P, BATCHES + 3, PARAMS], I32)
        params_src = sb("params_src", [P, BATCHES + 3, PARAMS], I32)
        flag = sb("flag", [1, 1], I32)
        g_earlier = sb("g_earlier", [CAP, CAP])
        g_trash = sb("g_trash", [CAP, 1])
        g_ones = sb("g_ones", [CAP, CAP])
        g_msg = sb("g_msg", [CAP, SUM])
        g_zero = sb("g_zero", [P, NT * SUM])
        edges = sb("edges", [CAP, COLS, 3], I32)
        w0t = sb("w0t", [P, P])
        wselft = sb("wselft", [P, P])
        wneit = sb("wneit", [P, P])
        w1 = sb("w1", [P, P])
        w2 = sb("w2", [P, P])
        wg_rec = sb("wg_rec", [P, P])
        wg_ws = sb("wg_ws", [P, 2 * P])
        wr = sb("wr", [P, P])
        eps_col = sb("eps_col", [P, 1])
        ones3 = sb("ones3", [3, P], BF16)
        bias0 = sb("bias0", [3, 4, P], BF16)
        bias1 = sb("bias1", [3, 4, P], BF16)
        bias3 = sb("bias3", [3, 4, P], BF16)
        biase = sb("biase", [3, 4, P], BF16)

        def pre(name, shape, dt=F32):
            return sb(name, shape, dt, early)

        dst_halo = pre("dst_halo", [CAP, SPAN], I32)
        dstf = pre("dstf", [CAP, SPAN])
        same = pre("same", [CAP, SPAN + 1])
        ones_row = pre("ones_row", [CAP, SPAN])
        fwd = pre("fwd", [CAP, SPAN])
        bwd = pre("bwd", [CAP, SPAN])
        inv_deg = pre("inv_deg", [CAP, COLS])
        falls = pre("falls", [CAP, COLS])
        bad = pre("bad", [CAP, 1])
        wid = pre("wid", [CAP, COLS], I32)
        wid_hi = pre("wid_hi", [CAP, COLS], I32)
        wid_lo = pre("wid_lo", [CAP, COLS], I32)
        iota32 = pre("iota32", [CAP, 32])
        count = pre("count", [HI, 32])
        upto = pre("upto", [HI, 32])
        low = pre("low", [HI, 32])
        over = pre("over", [HI, 32])
        bad_hi = pre("bad_hi", [HI, 1])
        rows_up = pre("rows_up", [HI, HI])
        ones_col = pre("ones_col", [P, 1])
        low_w = pre("low_w", [P, GROUPS])
        row0 = pre("row0", [P, GROUPS], I32)
        row0f = pre("row0f", [P, GROUPS])
        start = pre("start", [P, GROUPS])
        row1 = pre("row1", [P, GROUPS], I32)
        iota_slot = pre("iota_slot", [P, CAP])
        in0 = pre("in0", [P, GROUPS, CAP])
        in1 = pre("in1", [P, GROUPS, CAP])
        fetched_i = pre("fetched_i", [P, 2, 2, GROUPS, CAP], I32)
        fetched_f = pre("fetched_f", [P, 2, 2, GROUPS, CAP])
        part = pre("part", [P, 2, GROUPS, CAP])
        table = pre("table", [P, 4, GROUPS, CAP])
        win_base = pre("win_base", [P, WINDOWS])
        dtab = pre("dtab", [P, WINDOWS])
        inside = pre("inside", [P, WINDOWS])
        w_raw = pre("w_raw", [P, 3, P])
        b_raw = pre("b_raw", [3, 6, P])
        b_sum = pre("b_sum", [3, P])
        b_hi = pre("b_hi", [3, 6, P], BF16)
        b_mid = pre("b_mid", [3, 6, P], BF16)
        b_lo = pre("b_lo", [3, 6, P], BF16)
        b_r1 = pre("b_r1", [3, 6, P])
        b_r2 = pre("b_r2", [3, 6, P])
        b_mix = pre("b_mix", [3, 2, 6, P])
        iota_w = pre("iota_w", [CAP, WINDOWS], F16)
        r_earlier = pre("r_earlier", [CAP, CAP], F16)
        r_later = pre("r_later", [CAP, CAP], F16)
        r_all = pre("r_all", [CAP, CAP], F16)
        swid = pre("swid", [CAP, COLS], I32)
        swid_i = pre("swid_i", [CAP, COLS], I32)
        swidf = pre("swidf", [CAP, COLS + 1])
        r_scrap = pre("r_scrap", [CAP, 2, WUSED], F16)
        rank = pre("rank", [CAP, 2, GROUP])
        rank_max = pre("rank_max", [CAP, GROUP])
        rank_row = pre("rank_row", [CAP, GROUP])
        rank_win = pre("rank_win", [CAP, GROUP])
        aside = pre("aside", [CAP, GROUP])
        spare = pre("spare", [CAP, COLS])
        spill = pre("spill", [CAP, 1])
        place = pre("place", [CAP, 2, GROUP], I32)
        rec = pre("rec", [CAP, 2, GROUP, REC], I32)
        src_raw = pre("src_raw", [CAP, COLS], I32)
        ew_raw = pre("ew_raw", [CAP, COLS], I32)
        counting = ExitStack()
        is_hi = sb("is_hi", [CAP, COLS, HI], BF16, counting)
        is_lo = sb("is_lo", [CAP, COLS, 32], BF16, counting)
        counting.close()
        records = pre("records", [CAP, COLS, REC], I32)
        is_win = pre("is_win", [CAP, 4, WUSED], F16)
        src_table = pre("src_table", [P, WINDOWS, REC], I32)
        early.close()

        ep = sb("ep", [P, SLOTS, PARAMS], I32)
        rows = sb("rows", [P, SLOTS, 2 * NW, ROW])
        xn = sb("xn", [P, SLOTS, NT, ROW])
        xo = sb("xo", [P, SLOTS, NT, ROW])
        xh = sb("xh", [P, SLOTS, NT, P])
        sel = sb("sel", [P, SLOTS, NW * 2 * P])
        msg = sb("msg", [P, SLOTS, NW, P])
        scale = sb("scale", [P, SLOTS, NW])
        agg_t = sb("agg_t", [P, SLOTS, BATCH])
        h_t = sb("h_t", [P, SLOTS, BATCH])
        prod_t = sb("prod_t", [P, SLOTS, BATCH])
        eh = sb("eh", [P, SLOTS, 2 * NW, P])
        eh_t = sb("eh_t", [P, 2, 2 * NW, P])
        eta = sb("eta", [P, 2, NW, P])
        stat = sb("stat", [P, SLOTS, NT, 6])
        var = sb("var", [P, SLOTS, NT, 2])
        std = sb("std", [P, SLOTS, NT])
        estat = sb("estat", [P, SLOTS, NW, 6])
        evar = sb("evar", [P, SLOTS, NW, 2])
        estd = sb("estd", [P, SLOTS, NW])
        einv = sb("einv", [P, SLOTS, NW])
        enmi = sb("enmi", [P, SLOTS, NW])

        g_edge = sb("g_edge", [CAP, 3], I32)
        g_key = sb("g_key", [CAP, 1])
        g_diag = sb("g_diag", [CAP, CAP])
        g_same = sb("g_same", [CAP, CAP])
        g_before = sb("g_before", [CAP, CAP])
        g_prior = sb("g_prior", [CAP, 1])
        g_tof = sb("g_tof", [CAP, 1])
        g_to = sb("g_to", [CAP, 1], I32)
        g_total = sb("g_total", [CAP, SUM])
        g_sums = sb("g_sums", [P, NT, SUM])
        g_deg = sb("g_deg", [P, NT])
        g_mean = sb("g_mean", [P, NT, P])

        ps_e = ctx.enter_context(nc.psum_tensor("ps_e", [P, 1024], F32))
        ps_t = ctx.enter_context(nc.psum_tensor("ps_t", [P, 1024], F32))
        ps_o = ctx.enter_context(nc.psum_tensor("ps_o", [P, 2, 1024], F32))

        joined = sem("joined")
        moved = sem("moved")
        ALL = (0, 1, 2, 3)

        def ev(name, layers=ALL):
            return Event(sem(name), [l for l in layers if l in ALL], moved)

        def landed(name, per):
            return Landed([sem(f"{name}{s}") for s in range(SLOTS)], {l: v for l, v in per.items() if l in ALL}, moved)

        ep_in = landed("ep_in", {l: 16 for l in ALL})
        gathered = landed("gathered", {0: 64, 1: 64, 2: 64, 3: 128})
        x_in = landed("x_in", {l: 16 for l in ALL})
        x_stored = landed("x_stored", {l: 16 for l in ALL})
        x_tail = sem("x_tail")
        out_tail = sem("out_tail")
        e_stats = ev("e_stats", (0,))
        e_var = ev("e_var", (0,))
        e_std = ev("e_std", (0,))
        e_inv = ev("e_inv", (0,))
        e_nmi = ev("e_nmi", (0,))
        e_scale = ev("e_scale", (1, 2))
        e_norm = ev("e_norm", (0, 1, 3))
        e_normd = ev("e_normd", (1, 2, 3))
        e_sel = ev("e_sel")
        e_tr = ev("e_tr", (3,))
        e_ht = ev("e_ht", (3,))
        e_gate = ev("e_gate", (3,))
        e_eta = ev("e_eta", (3,))
        e_msg = ev("e_msg", (3,))
        e_agg = ev("e_agg", (0, 1, 2))
        n_aggt = ev("n_aggt", (0, 1, 2))
        n_norm = ev("n_norm", (1, 2, 3))
        n_tr = ev("n_tr", (1, 2, 3))
        n_ht = ev("n_ht", (1, 3))
        n_prod = ev("n_prod", (2,))
        n_mm = ev("n_mm")
        n_out = ev("n_out")
        n_stats = ev("n_stats", (0, 1, 2))
        n_var = ev("n_var", (0, 1, 2))
        n_std = ev("n_std", (0, 1, 2))
        n_inv = ev("n_inv", (0, 1, 2))
        n_mean = ev("n_mean", (0, 1, 2))
        n_fin = ev("n_fin", (0, 1, 2))

        g_edge_in = sem("g_edge_in")
        g_rows_in = sem("g_rows_in")
        g_zeroed = sem("g_zeroed")
        g_added = sem("g_added")
        g_diagd = sem("g_diagd")
        g_keys = sem("g_keys")
        g_var = sem("g_var")
        g_std = sem("g_std")
        g_hd = sem("g_hd")
        g_tr = sem("g_tr")
        g_ht = sem("g_ht")
        g_gate = sem("g_gate")
        g_eta = sem("g_eta")
        g_msgd = sem("g_msgd")
        g_comb = sem("g_comb")
        g_totald = sem("g_totald")
        g_step = sem("g_step")
        gn_in = sem("gn_in")
        gn_sums_in = sem("gn_sums_in")
        gn_stored = sem("gn_stored")
        gn_var = sem("gn_var")
        gn_std = sem("gn_std")
        gn_ready = sem("gn_ready")
        gn_tr = sem("gn_tr")
        gn_take = sem("gn_take")
        gn_prod = sem("gn_prod")
        gn_mm = sem("gn_mm")
        gn_out = sem("gn_out")
        gn_step = sem("gn_step")

        def join(eng, k):
            eng.drain().then_inc(joined, 1)
            eng.wait_ge(joined, 5 * k)

        p_rows = sem("p_rows")
        p_dst = [sem("p_dst0"), sem("p_dst1"), sem("p_dst2")]
        p_w = sem("p_w")
        p_raw = sem("p_raw")
        p_halo = sem("p_halo")
        p_inv = sem("p_inv")
        p_invd = sem("p_invd")
        p_low = sem("p_low")
        p_lowd = sem("p_lowd")
        p_lowin = sem("p_lowin")
        p_pool = sem("p_pool")
        p_fetch = sem("p_fetch")
        p_onehot = sem("p_onehot")
        p_count = sem("p_count")
        p_upto = sem("p_upto")
        p_rank = sem("p_rank")
        p_wt = sem("p_wt")
        p_tab = sem("p_tab")
        p_tabt = sem("p_tabt")
        p_tabc = sem("p_tabc")
        p_step = sem("p_step")

        r_const = sem("r_const")
        r_empty = sem("r_empty")
        r_blank = sem("r_blank")
        r_records = sem("r_records")
        r_win = sem("r_win")
        r_mm = sem("r_mm")
        r_rank = sem("r_rank")
        r_step = sem("r_step")
        r_place = sem("r_place")
        r_rec_in = [sem("r_rec_in0"), sem("r_rec_in1")]
        r_out = [sem("r_out0"), sem("r_out1")]
        r_table_in = sem("r_table_in")
        r_spill = sem("r_spill")
        r_spilled = sem("r_spilled")

        GROUPS_OF_TILES = TILES // GROUP

        def sp_rank(sp):
            sp.wait_ge(r_empty, 1)
            sp.dma_start(by_src[0:LAST_RANK * WINDOWS, :].rearrange("(p c) d -> p (c d)", p=P),
                         src_table[:].rearrange("p c d -> p (c d)")).then_inc(r_blank, 16)
            sp.wait_ge(r_records, 1)
            for u in range(2):
                sp.dma_start(rec[:, u].rearrange("p k d -> p (k d)"),
                             records[:, GROUP * u:GROUP * (u + 1), :].rearrange("p k d -> p (k d)")
                             ).then_inc(r_rec_in[u], 16)
            with sp.Fori(1, GROUPS_OF_TILES // 2) as i:
                for u in range(2):
                    sp.wait_ge(r_out[u], 16 * GROUP * i)
                    settle(sp, moved)
                    sp.dma_start(rec[:, u].rearrange("p k d -> p (k d)"),
                                 records[:, bass.ds(2 * GROUP * i + GROUP * u, GROUP), :].rearrange("p k d -> p (k d)")
                                 ).then_inc(r_rec_in[u], 16)
            for u in range(2):
                sp.wait_ge(r_out[u], 16 * GROUP * (GROUPS_OF_TILES // 2))
            sp.dma_start(src_table[:].rearrange("p c d -> p (c d)"),
                         by_src[0:LAST_RANK * WINDOWS, :].rearrange("(p c) d -> p (c d)", p=P)).then_inc(r_table_in, 16)
            sp.wait_ge(r_table_in, 16)

        def pool_rank(pool):
            def body(i, u):
                pool.wait_ge(r_place, 2 * i + u + 1)
                pool.wait_ge(r_rec_in[u], 16 * i + 16)
                settle(pool, moved)
                for k in range(GROUP):
                    nc.gpsimd.indirect_dma_start(
                        by_src, bass.IndirectOffsetOnAxis(ap=place[:, u, k:k + 1], axis=0), rec[:, u, k, :], None
                    ).then_inc(r_out[u], 16)

            pool.wait_ge(r_blank, 16)
            with pool.Fori(0, GROUPS_OF_TILES // 2) as i:
                for u in range(2):
                    body(i, u)

        def pe_rank(pe):
            def add(u, mat, q, start, stop):
                for a, b in ((0, 512), (512, WUSED)):
                    mm = pe.matmul(ps_o[0:CAP, u, a:b], mat[:], is_win[:, q, a:b], start=start, stop=stop,
                                   skip_group_check=True)
                return mm

            def body(t, c, first):
                pe.wait_ge(r_win, t + 1)
                if c > 1 or not first:
                    pe.wait_ge(r_rank, t - 1)
                    add(c % 2, r_later, (c - 2) % 4, False, False)
                if c > 0 or not first:
                    add(c % 2, r_all, (c - 1) % 4, first and c == 1, False)
                add(c % 2, r_earlier, c % 4, first and c == 0, True).then_inc(r_mm, 1)

            pe.wait_ge(r_const, 7)
            for c in range(4):
                body(c, c, True)
            with pe.Fori(1, TILES // 4) as i:
                for c in range(4):
                    body(4 * i + c, c, False)

        def dve_rank(dve):
            v = nc.vector

            def windows_of(t, c, first):
                if not first:
                    dve.wait_ge(r_mm, t - 1)
                v.tensor_scalar(is_win[:, c % 4, :], iota_w[:, 0:WUSED],
                                swidf[:, t:t + 1] if isinstance(t, int) else swidf[:, bass.ds(t, 1)], None,
                                ALU.is_equal).then_inc(r_win, 1)

            def take_rank(t, c):
                if not isinstance(t, int) or t > 1:
                    dve.wait_ge(r_rank, t - 1)
                dve.wait_ge(r_mm, t + 1)
                v.tensor_tensor_reduce(out=r_scrap[:, c % 2, :], in0=ps_o[0:CAP, c % 2, 0:WUSED], in1=is_win[:, c % 4, :],
                                       scale=1.0, scalar=0.0, op0=ALU.mult, op1=ALU.add,
                                       accum_out=rank[:, c // 4 % 2, c % 4:c % 4 + 1]).then_inc(r_rank, 1)

            def place_a(g, u):
                if not isinstance(g, int) or g > 0:
                    dve.wait_ge(r_place, g)
                dve.wait_ge(r_rank, GROUP * g + GROUP)
                v.tensor_tensor(rank_max[:], rank_max[:], rank[:, u], ALU.max).then_inc(r_step, 1)
                v.tensor_scalar(rank_row[:], rank[:, u], float(LAST_RANK), float(WINDOWS), ALU.min, ALU.mult
                                ).then_inc(r_step, 1)
                v.scalar_tensor_tensor(out=aside[:], in0=rank[:, u], scalar=float(LAST_RANK), in1=spare[:, own(g)],
                                       op0=ALU.is_ge, op1=ALU.mult).then_inc(r_step, 1)

            def place_b(g):
                dve.wait_ge(r_step, 4 * g + 3)
                v.tensor_tensor(rank_win[:], rank_row[:], swidf[:, own(g)], ALU.add).then_inc(r_step, 1)

            def place_c(g, u, i):
                if not isinstance(i, int) or i > 0:
                    dve.wait_ge(r_out[u], 16 * GROUP * i)
                dve.wait_ge(r_step, 4 * g + 4)
                v.tensor_tensor(place[:, u, :], rank_win[:], aside[:], ALU.add).then_inc(r_place, 1)

            def own(g):
                return slice(GROUP * g, GROUP * (g + 1)) if isinstance(g, int) else bass.ds(GROUP * g, GROUP)

            windows_of(0, 0, True)
            windows_of(1, 1, True)
            for t in range(1, 16):
                g, c = t // GROUP - 1, t % GROUP
                take_rank(t - 1, t - 1)
                if c == 1 and g >= 0:
                    place_b(g)
                windows_of(t + 1, t + 1, t < 3)
                if c == 0:
                    place_a(g, g % 2)
                if c == 1 and g >= 0:
                    place_c(g, g % 2, g // 2)
            with dve.Fori(2, TILES // 8) as i:
                for c in range(8):
                    take_rank(8 * i + c - 1, (c - 1) % 8)
                    if c == 1:
                        place_b(2 * i - 1)
                    if c == 5:
                        place_b(2 * i)
                    windows_of(8 * i + c + 1, c + 1, False)
                    if c == 0:
                        place_a(2 * i - 1, 1)
                    if c == 4:
                        place_a(2 * i, 0)
                    if c == 1:
                        place_c(2 * i - 1, 1, i - 1)
                    if c == 5:
                        place_c(2 * i, 0, i)
            take_rank(TILES - 1, TILES - 1)
            place_a(GROUPS_OF_TILES - 1, 1)
            place_b(GROUPS_OF_TILES - 1)
            place_c(GROUPS_OF_TILES - 1, 1, GROUPS_OF_TILES // 2 - 1)
            dve.wait_ge(r_step, 4 * GROUPS_OF_TILES)

        dst_rows = dst.rearrange("(p c) -> p c", c=COLS)
        edge_rows = [src.rearrange("(r c) -> r c", c=CAP), dst.rearrange("(r c) -> r c", c=CAP),
                     edge_weight.rearrange("(r c) -> r c", c=CAP), inv_dram.rearrange("(r c) -> r c", c=CAP)]

        def sp_prepare(sp):
            sp.dma_start(dst_halo[:, HALO:HALO + COLS], dst_rows).then_inc(p_dst[0], 16)
            sp.wait_ge(p_halo, 1)
            sp.dma_start(dst_halo[1:CAP, 0:HALO], dst_rows[0:CAP - 1, COLS - HALO:COLS]).then_inc(p_dst[1], 16)
            sp.dma_start(dst_halo[0:CAP - 1, HALO + COLS:SPAN], dst_rows[1:CAP, 0:HALO]).then_inc(p_dst[2], 16)
            sp.dma_start(src_raw[:], src.rearrange("(p c) -> p c", c=COLS)).then_inc(p_raw, 16)
            sp.dma_start(ew_raw[:], edge_weight.bitcast(I32).rearrange("(p c) -> p c", c=COLS)).then_inc(p_raw, 16)
            for k, w in enumerate((W0, W_self, W_nei)):
                sp.dma_start(w_raw[:, k, :], w).then_inc(p_w, 16)
            sp.dma_start(w1[:], W1).then_inc(p_w, 16)
            sp.dma_start(w2[:], W2).then_inc(p_w, 16)
            sp.dma_start(wg_rec[:], Wg[0:P, :]).then_inc(p_w, 16)
            sp.dma_start(wg_ws[:, 0:P], Wg[P:2 * P, :]).then_inc(p_w, 16)
            sp.dma_start(wg_ws[:, P:2 * P], Ws).then_inc(p_w, 16)
            sp.dma_start(wr[:], Wr).then_inc(p_w, 16)
            for k, b in enumerate((b0, b_self, b_nei, bg, bs, br)):
                one = b.rearrange("(a f) -> a f", a=1)
                for q in range(3):
                    sp.dma_start(b_raw[q:q + 1, k, :], one).then_inc(p_w, 16)
            sp.wait_ge(p_inv, 1)
            sp.dma_start(inv_dram.rearrange("(p c) -> p c", c=COLS), inv_deg[:]).then_inc(p_invd, 16)
            sp.wait_ge(p_low, 1)
            sp.dma_start(low_dram.rearrange("(h l) -> h l", l=32), low[:]).then_inc(p_lowd, 16)
            sp.wait_ge(p_lowd, 16)
            with nc.allow_non_contiguous_dma(reason="640 words once"):
                sp.dma_start(low_w[:], low_dram.rearrange("(g p) -> p g", p=P)).then_inc(p_lowin, 16)
            sp.wait_ge(p_lowin, 16)
            sp.wait_ge(p_invd, 16)
            sp.wait_ge(p_w, 16 * 27)
            sp_rank(sp)

        def pool_prepare(pool):
            g = nc.gpsimd
            g.iota(iota_w[:], pattern=[[1, WINDOWS]], base=0, channel_multiplier=0,
                   allow_small_or_imprecise_dtypes=True).then_inc(r_const, 1)
            g.memset(r_earlier[:], 1.0).then_inc(r_const, 1)
            g.memset(r_later[:], 1.0).then_inc(r_const, 1)
            g.memset(r_all[:], 1.0).then_inc(r_const, 1)
            g.iota(spare[:], pattern=[[1, COLS]], base=0, channel_multiplier=COLS,
                   allow_small_or_imprecise_dtypes=True).then_inc(r_const, 1)
            pool.wait_ge(r_const, 5)
            g.affine_select(out=r_earlier[:], in_=r_earlier[:], compare_op=ALU.is_gt, fill=0.0, base=0,
                            pattern=[[1, CAP]], channel_multiplier=-1).then_inc(r_const, 1)
            g.affine_select(out=r_later[:], in_=r_later[:], compare_op=ALU.is_ge, fill=0.0, base=0,
                            pattern=[[-1, CAP]], channel_multiplier=1).then_inc(r_const, 1)
            g.memset(ident[:], 0.0).then_inc(p_pool, 1)
            pool.wait_ge(p_pool, 1)
            g.affine_select(out=ident[:], in_=ident[:], compare_op=ALU.not_equal, fill=1.0, base=0,
                            pattern=[[-1, P]], channel_multiplier=1).then_inc(p_pool, 1)
            g.iota(iota_win[:], pattern=[[0, NW], [1, WIN]], base=0, channel_multiplier=0,
                   allow_small_or_imprecise_dtypes=True).then_inc(p_pool, 1)
            g.iota(iota_pair[:], pattern=[[P - WIN, NW], [1, 2 * P]], base=0, channel_multiplier=0,
                   allow_small_or_imprecise_dtypes=True).then_inc(p_pool, 1)
            g.iota(iota32[:], pattern=[[1, 32]], base=0, channel_multiplier=0,
                   allow_small_or_imprecise_dtypes=True).then_inc(p_pool, 1)
            g.iota(iota_slot[:], pattern=[[1, CAP]], base=0, channel_multiplier=0,
                   allow_small_or_imprecise_dtypes=True).then_inc(p_pool, 1)
            g.iota(win_base[:], pattern=[[WIN, WINDOWS]], base=0, channel_multiplier=0,
                   allow_small_or_imprecise_dtypes=True).then_inc(p_pool, 1)
            g.memset(rows_up[:], 1.0).then_inc(p_pool, 1)
            g.iota(g_trash[:], pattern=[[0, 1]], base=TRASH, channel_multiplier=1,
                   allow_small_or_imprecise_dtypes=True).then_inc(p_pool, 1)
            g.memset(g_earlier[:], 1.0).then_inc(p_pool, 1)
            pool.wait_ge(p_pool, 10)
            g.affine_select(out=g_earlier[:], in_=g_earlier[:], compare_op=ALU.is_gt, fill=0.0, base=0,
                            pattern=[[-1, CAP]], channel_multiplier=1).then_inc(p_pool, 1)
            g.affine_select(out=rows_up[:], in_=rows_up[:], compare_op=ALU.is_gt, fill=0.0, base=0,
                            pattern=[[1, HI]], channel_multiplier=-1).then_inc(p_pool, 1)
            pool.wait_ge(p_rows, 1)
            for f in range(3):
                to = fetched_i[:, f] if f < 2 else fetched_f[:, 0]
                for k, at in enumerate((row0, row1)):
                    for q in range(GROUPS):
                        g.indirect_dma_start(to[:, k, q, :], None, edge_rows[f], bass.IndirectOffsetOnAxis(
                            ap=at[:, q:q + 1], axis=0)).then_inc(p_fetch, 16)
            pool.wait_ge(p_invd, 16)
            for k, at in enumerate((row0, row1)):
                for q in range(GROUPS):
                    g.indirect_dma_start(fetched_f[:, 1, k, q, :], None, edge_rows[3], bass.IndirectOffsetOnAxis(
                        ap=at[:, q:q + 1], axis=0)).then_inc(p_fetch, 16)

            pool_rank(pool)

        def act_prepare(act):
            pass

        def pe_prepare(pe):
            pe.wait_ge(p_pool, 12)
            pe.wait_ge(p_w, 16 * 27)
            for k in range(3):
                mm = pe.transpose(ps_t[:, k * P:(k + 1) * P], w_raw[:, k, :], ident[:])
            mm.then_inc(p_wt, 1)
            pe.wait_ge(p_onehot, 2)
            for c in range(COLS):
                mm = pe.matmul(ps_o[0:HI, 0, 0:32], is_hi[:, c, :], is_lo[:, c, :], start=(c == 0), stop=(c == COLS - 1))
            mm.then_inc(p_count, 1)
            pe.wait_ge(p_upto, 1)
            pe.matmul(ps_o[0:HI, 1, 0:1], rows_up[:], upto[:, 31:32], start=True, stop=True).then_inc(p_rank, 1)
            pe.wait_ge(p_upto, 2)
            pe.matmul(ps_e[0:1, 0:1], bad[:], ones_col[0:CAP, :], start=True, stop=False)
            pe.matmul(ps_e[0:1, 0:1], bad_hi[:], ones_col[0:HI, :], start=False, stop=False)
            pe_rank(pe)
            pe.wait_ge(r_spill, 1)
            pe.matmul(ps_e[0:1, 0:1], spill[:], ones_col[0:CAP, :], start=False, stop=True).then_inc(r_spilled, 1)
            for f in range(4):
                pe.wait_ge(p_tab, f + 1)
                if f:
                    pe.wait_ge(p_tabc, f)
                for q in range(GROUPS):
                    mm = pe.transpose(ps_t[0:CAP, q * P:(q + 1) * P], table[:, f, q, :], ident[:])
                mm.then_inc(p_tabt, 1)

        def dve_prepare(dve):
            v = nc.vector
            n = [0]

            def done(ins):
                n[0] += 1
                ins.then_inc(p_step, 1)
                dve.wait_ge(p_step, n[0])

            v.memset(dst_halo[:, 0:HALO], -1)
            v.memset(dst_halo[:, HALO + COLS:SPAN], 1 << 20).then_inc(p_halo, 1)
            v.memset(params_src[:], 0)
            v.memset(eps_col[:], EPS)
            v.memset(ones3[:], 1.0)
            v.memset(ones_col[:], 1.0)
            v.memset(same[:], 0.0)
            v.memset(params[:], 0)
            done(v.memset(ones_row[:], 1.0))
            v.memset(g_ones[:], 1.0)
            v.memset(g_msg[:], 1.0)
            v.memset(g_zero[:], 0.0)
            for s in p_dst:
                dve.wait_ge(s, 16)
            v.tensor_copy(edges[:, :, 1], dst_halo[:, HALO:HALO + COLS])
            dve.wait_ge(p_raw, 32)
            v.tensor_copy(edges[:, :, 0], src_raw[:])
            v.tensor_copy(edges[:, :, 2], ew_raw[:])
            done(v.tensor_copy(dstf[:], dst_halo[:]))
            done(v.tensor_tensor(same[:, 1:SPAN], dstf[:, 1:SPAN], dstf[:, 0:SPAN - 1], ALU.is_equal))
            v.tensor_tensor_scan(fwd[:], same[:, 0:SPAN], ones_row[:], 0.0, ALU.mult, ALU.add)
            done(v.tensor_tensor_scan(bwd[:, ::-1], same[:, 1:SPAN + 1][:, ::-1], ones_row[:], 0.0, ALU.mult, ALU.add))
            done(v.scalar_tensor_tensor(out=inv_deg[:], in0=fwd[:, HALO:HALO + COLS], scalar=-1.0,
                                        in1=bwd[:, HALO:HALO + COLS], op0=ALU.add, op1=ALU.add))
            v.reciprocal(inv_deg[:], inv_deg[:]).then_inc(p_inv, 1)
            done(v.tensor_tensor(falls[:], dstf[:, HALO:HALO + COLS], dstf[:, HALO - 1:HALO + COLS - 1], ALU.is_lt))
            v.tensor_reduce(bad[:], falls[:], AX.X, ALU.max)
            done(v.tensor_scalar(wid[:], dst_halo[:, HALO:HALO + COLS], 5, None, ALU.arith_shift_right))
            done(v.tensor_scalar(wid_hi[:], wid[:], 0.2, -0.4, ALU.mult, ALU.add))
            v.tensor_scalar(wid_lo[:], wid_hi[:], 31, None, ALU.bitwise_and)
            done(v.tensor_scalar(wid[:], wid_hi[:], 5, None, ALU.arith_shift_right))
            dve.wait_ge(p_pool, 12)
            v.tensor_tensor(is_hi[:], wid[:].rearrange("p (c a) -> p c a", a=1).to_broadcast([CAP, COLS, HI]),
                            iota32[:, 0:HI].rearrange("p (a h) -> p a h", a=1).to_broadcast([CAP, COLS, HI]),
                            ALU.is_equal).then_inc(p_onehot, 1)
            v.tensor_tensor(is_lo[:], wid_lo[:].rearrange("p (c a) -> p c a", a=1).to_broadcast([CAP, COLS, 32]),
                            iota32[:].rearrange("p (a h) -> p a h", a=1).to_broadcast([CAP, COLS, 32]),
                            ALU.is_equal).then_inc(p_onehot, 1)
            dve.wait_ge(p_w, 16 * 27)
            done(v.tensor_tensor(b_sum[:], b_raw[:, 1, :], b_raw[:, 2, :], ALU.add))
            done(v.tensor_copy(b_raw[:, 1, :], b_sum[:]))
            done(v.tensor_copy(b_hi[:], b_raw[:]))
            done(v.tensor_tensor(b_r1[:], b_raw[:], b_hi[:], ALU.subtract))
            done(v.tensor_copy(b_mid[:], b_r1[:]))
            done(v.tensor_tensor(b_r2[:], b_r1[:], b_mid[:], ALU.subtract))
            done(v.tensor_copy(b_lo[:], b_r2[:]))
            done(v.tensor_scalar(b_mix[:, 0], b_hi[:], ident[0:3, 0:1], None, ALU.mult))
            done(v.scalar_tensor_tensor(out=b_mix[:, 1], in0=b_mid[:], scalar=ident[0:3, 1:2], in1=b_mix[:, 0],
                                        op0=ALU.mult, op1=ALU.add))
            done(v.scalar_tensor_tensor(out=b_mix[:, 0], in0=b_lo[:], scalar=ident[0:3, 2:3], in1=b_mix[:, 1],
                                        op0=ALU.mult, op1=ALU.add))
            for q in range(4):
                v.tensor_copy(bias0[:, q, :], b_mix[:, 0, 0, :])
                v.tensor_copy(bias1[:, q, :], b_mix[:, 0, 1, :])
                v.tensor_copy(biase[:, q, :], b_mix[:, 0, 3 + q % 2, :])
                v.tensor_copy(bias3[:, q, :], b_mix[:, 0, 5, :])
            dve.wait_ge(p_wt, 1)
            v.tensor_copy(w0t[:], ps_t[:, 0:P])
            v.tensor_copy(wselft[:], ps_t[:, P:2 * P])
            done(v.tensor_copy(wneit[:], ps_t[:, 2 * P:3 * P]))
            dve.wait_ge(p_count, 1)
            done(v.tensor_copy(count[:], ps_o[0:HI, 0, 0:32]))
            done(v.memset(src_table[:], 0))
            done(v.memset(src_table[:].bitcast(F32)[:, :, 1], NOWHERE))
            dve.sem_inc(r_empty, 1)
            v.tensor_tensor_scan(upto[:], ones_row[0:HI, 0:32], count[:], 0.0, ALU.mult, ALU.add).then_inc(p_upto, 1)
            done(v.tensor_scalar(over[:], count[:], float(CAP), None, ALU.is_gt))
            done(v.tensor_reduce(bad_hi[:], over[:], AX.X, ALU.max))
            done(v.tensor_tensor(low[:], upto[:], count[:], ALU.subtract))
            dve.wait_ge(p_rank, 1)
            v.tensor_copy(over[:, 0:1], ps_o[0:HI, 1, 0:1]).then_inc(p_upto, 1)
            dve.wait_ge(p_upto, 2)
            v.tensor_scalar(low[:], low[:], over[:, 0:1], None, ALU.add).then_inc(p_low, 1)
            dve.wait_ge(p_lowin, 16)
            done(v.tensor_scalar(row0[:], low_w[:], 1.0 / CAP, -(CAP // 2) / CAP, ALU.mult, ALU.add))
            done(v.tensor_scalar(row0f[:], row0[:], float(EROWS - 1), None, ALU.min))
            v.tensor_copy(row0[:], row0f[:])
            v.tensor_scalar(row1[:], row0f[:], 1.0, float(EROWS - 1), ALU.add, ALU.min).then_inc(p_rows, 1)
            done(v.scalar_tensor_tensor(out=start[:], in0=row0f[:], scalar=-float(CAP), in1=low_w[:],
                                        op0=ALU.mult, op1=ALU.add))
            for q in range(GROUPS):
                v.tensor_scalar(in0[:, q, :], iota_slot[:], start[:, q:q + 1], None, ALU.is_ge)
                v.tensor_scalar(in1[:, q, :], iota_slot[:], start[:, q:q + 1], None, ALU.is_lt)
            done(v.memset(dtab[:], 0.0))
            v.memset(rank_max[:], 0.0)
            v.memset(records[:], 0)
            done(v.tensor_scalar(swid[:], src_raw[:], 5, None, ALU.arith_shift_right))
            done(v.tensor_scalar(swid_i[:], swid[:], 0.2, -0.4, ALU.mult, ALU.add))
            v.memset(swidf[:, COLS:COLS + 1], -1.0)
            done(v.tensor_copy(swidf[:, 0:COLS], swid_i[:]))
            v.scalar_tensor_tensor(out=records[:].bitcast(F32)[:, :, 1], in0=swidf[:, 0:COLS], scalar=-float(WIN),
                                   in1=src_raw[:], op0=ALU.mult, op1=ALU.add)
            dve.wait_ge(r_const, 7)
            v.tensor_tensor(spare[:], spare[:], swidf[:, 0:COLS], ALU.subtract)
            v.tensor_copy(records[:, :, 0], dst_halo[:, HALO:HALO + COLS])
            done(v.tensor_copy(records[:, :, 2], ew_raw[:]))
            dve.sem_inc(r_records, 1)
            dve_rank(dve)
            done(v.tensor_reduce(spill[:], rank_max[:], AX.X, ALU.max))
            v.tensor_scalar(spill[:], spill[:], float(LAST_RANK), None, ALU.is_ge).then_inc(r_spill, 1)
            dve.wait_ge(r_spilled, 1)
            done(v.tensor_scalar(flag[:], ps_e[0:1, 0:1], 1.0, None, ALU.min))
            dve.wait_ge(p_fetch, 16 * 8 * GROUPS)
            for f in range(4):
                a = fetched_i[:, f] if f < 2 else fetched_f[:, f - 2]
                v.tensor_tensor(part[:, 0], a[:, 0], in0[:], ALU.mult)
                done(v.tensor_tensor(part[:, 1], a[:, 1], in1[:], ALU.mult))
                done(v.tensor_tensor(table[:, f], part[:, 0], part[:, 1], ALU.add))
                dve.sem_inc(p_tab, 1)
            to = params[:].bitcast(F32)
            wins = BATCHES * NW

            def column(tab, at):
                return tab[0:CAP, 0:BATCHES, at:at + NW]

            def windows(ap):
                return ap[0:CAP, 0:wins].rearrange("p (n k) -> p n k", k=NW)

            dve.wait_ge(p_tabt, 1)
            v.tensor_copy(column(params, SRC), windows(ps_t)).then_inc(p_tabc, 1)
            dve.wait_ge(p_tabt, 2)
            v.tensor_copy(column(params, DST), windows(ps_t))
            done(v.tensor_tensor(dtab[0:CAP, :], ps_t[0:CAP, 0:WINDOWS], win_base[0:CAP, :], ALU.subtract))
            dve.sem_inc(p_tabc, 1)
            done(v.tensor_scalar(inside[0:CAP, :], dtab[0:CAP, :], 0.0, None, ALU.is_ge))
            done(v.scalar_tensor_tensor(out=inside[0:CAP, :], in0=dtab[0:CAP, :], scalar=float(WIN),
                                        in1=inside[0:CAP, :], op0=ALU.is_lt, op1=ALU.mult))
            done(v.scalar_tensor_tensor(out=dtab[0:CAP, :], in0=dtab[0:CAP, :], scalar=-NOWHERE,
                                        in1=inside[0:CAP, :], op0=ALU.add, op1=ALU.mult))
            done(v.memset(to[:, :, LOC:LOC + NW], NOWHERE))
            v.tensor_scalar(column(to, LOC), windows(dtab), NOWHERE, None, ALU.add)
            dve.wait_ge(p_tabt, 3)
            v.tensor_copy(column(to, EWT), windows(ps_t)).then_inc(p_tabc, 1)
            dve.wait_ge(p_tabt, 4)
            done(v.tensor_copy(column(to, DEG), windows(ps_t)))
            dve.wait_ge(r_table_in, 16)
            by_window = src_table[:, 0:WUSED, :].rearrange("p (n k) d -> p n k d", k=NW)
            for f, at in enumerate((SRC, LOC, EWT)):
                last = v.tensor_copy(params_src[:, 0:BATCHES, at:at + NW], by_window[:, :, :, f])
            done(last)
            done(v.memset(rows[96:P], 0.0))

        def node_rows(l, n):
            return nodes[l][bass.ds(BATCH * n, BATCH), :].rearrange("(r p) c -> p r c", p=P)

        def edge_params(b, at, n=NW):
            return ep[:, b.slot, at:at + n].bitcast(F32)

        def sp_layer(sp, l):
            store = STORE[l]
            width = P if l == 0 else ROW

            def body(t):
                b = t
                if b.real:
                    gathered.wait(sp, l, b.back(SLOTS))
                    e_sel.wait(sp, l, b.back(SLOTS))
                    if l in (1, 2):
                        e_scale.wait(sp, l, b.back(SLOTS))
                    table = params_src if l == 2 else params
                    sp.dma_start(ep[:, b.slot, :], table[:, bass.ds(b.n, 1), :].rearrange("p a c -> p (a c)")
                                 ).then_inc(ep_in.sems[b.slot], 16)
                b = t.back(X_LATER[l])
                if b.real:
                    n_out.wait(sp, l, b.back(SLOTS))
                    if l:
                        n_norm.wait(sp, l, b.back(SLOTS))
                    if l == 0 and isinstance(b.n, int) and b.n == BATCHES - 1:
                        sp.dma_start(xn[:, b.slot, 0, 0:P], x[NODES - TAIL:NODES - TAIL + P, :]
                                     ).then_inc(x_in.sems[b.slot], 16)
                        sp.dma_start(xn[0:TAIL - P, b.slot, 1, 0:P], x[NODES - TAIL + P:NODES, :]
                                     ).then_inc(x_tail, 16)
                    else:
                        sp.dma_start(xn[:, b.slot, :, 0:width], node_rows(l, b.n)).then_inc(x_in.sems[b.slot], 16)
                b = t.back(store)
                if not b.real:
                    return
                if l < 3:
                    n_fin.wait(sp, l, b)
                    if l == 0:
                        n_out.wait(sp, l, b)
                    sp.dma_start(node_rows(l + 1, b.n), xo[:, b.slot]).then_inc(x_stored.sems[b.slot], 16)
                else:
                    n_out.wait(sp, l, b)
                    if isinstance(b.n, int) and b.n == BATCHES - 1:
                        sp.dma_start(out[NODES - TAIL:NODES - TAIL + P, :], xo[:, b.slot, 0, 0:P]
                                     ).then_inc(x_stored.sems[b.slot], 16)
                        sp.dma_start(out[NODES - TAIL + P:NODES, :], xo[0:TAIL - P, b.slot, 1, 0:P]
                                     ).then_inc(out_tail, 16)
                        sp.wait_ge(out_tail, 16)
                    else:
                        sp.dma_start(out[bass.ds(BATCH * b.n, BATCH), :].rearrange("(r p) c -> p r c", p=P),
                                     xo[:, b.slot, :, 0:P]).then_inc(x_stored.sems[b.slot], 16)

            steps(sp, store, body)
            x_stored.all(sp, l)

        def pool_layer(pool, l):
            width = P if l == 0 else ROW
            used = P if l == 2 else CAP

            def body(b):
                ep_in.wait(pool, l, b)
                if l != 2:
                    e_norm.wait(pool, l, b.back(SLOTS))
                if l in (1, 2):
                    e_scale.wait(pool, l, b.back(SLOTS))
                if l:
                    e_normd.wait(pool, l, b.back(SLOTS))
                settle(pool, moved)
                for k in range(2 * NW if l == 3 else NW):
                    nc.gpsimd.indirect_dma_start(
                        rows[0:used, b.slot, k, 0:width], None, nodes[l],
                        bass.IndirectOffsetOnAxis(ap=ep[0:used, b.slot, k:k + 1], axis=0)
                    ).then_inc(gathered.sems[b.slot], 16)

            steps(pool, 0, body)

        def add_update(dve, l, b):
            s = b.slot
            n_mm.wait(dve, l, b)
            x_in.wait(dve, l, b)
            x_stored.wait(dve, l, b.back(SLOTS))
            if l == 1:
                nc.vector.scalar_tensor_tensor(out=xo[:, s, :, 0:P], in0=update(l, b), scalar=0.0,
                                               in1=xn[:, s, :, 0:P], op0=ALU.max, op1=ALU.add
                                               ).then_inc(n_out.sem, 1)
            else:
                nc.vector.tensor_tensor(xo[:, s, :, 0:P], update(l, b), xn[:, s, :, 0:P], ALU.add
                                        ).then_inc(n_out.sem, 1)

        def row_stats(dve, l, b):
            s = b.slot
            n_out.wait(dve, l, b)
            for r in range(NT):
                last = nc.vector.bn_stats(stat[:, s, r, :], xo[:, s, r, 0:P])
            last.then_inc(n_stats.sem, 1)

        def row_means(dve, l, b):
            s = b.slot
            n_stats.wait(dve, l, b)
            n_std.wait(dve, l, b.back(SLOTS))
            settle(dve, moved)
            for r in range(NT):
                last = nc.vector.bn_aggr(var[:, s, r, :], stat[:, s, r, :])
            last.then_inc(n_var.sem, 1)

        def update(l, b):
            return ps_o[:, 0 if l == 3 else b.c % 2, 0:BATCH].rearrange("p (r f) -> p r f", f=P)

        def row_inverses(dve, l, b):
            s = b.slot
            n_std.wait(dve, l, b)
            if l == 0:
                x_stored.wait(dve, l, b.back(SLOTS))
            nc.vector.reciprocal(xo[:, s, :, INV], std[:, s, :]).then_inc(n_inv.sem, 1)
            if l != 2:
                nc.vector.tensor_scalar(xo[:, s, :, NMEAN], var[:, s, :, 0], -1.0, None, ALU.mult
                                        ).then_inc(n_mean.sem, 1)

        def row_last(dve, l, b):
            s = b.slot
            n_inv.wait(dve, l, b)
            n_mean.wait(dve, l, b)
            nc.vector.tensor_tensor(xo[:, s, :, NMI], xo[:, s, :, NMEAN], xo[:, s, :, INV], ALU.mult
                                    ).then_inc(n_fin.sem, 1)

        def dve_layer(dve, l):
            v = nc.vector

            def body0(t):
                new, summed, old, e, f = t.back(5), t.back(6), t.back(7), t.back(2), t.back(3)
                if f.real:
                    s = f.slot
                    e_std.wait(dve, l, f)
                    e_norm.wait(dve, l, f.back(SLOTS))
                    v.reciprocal(einv[:, s, :], estd[:, s, :]).then_inc(e_inv.sem, 1)
                if summed.real:
                    row_means(dve, l, summed)
                if f.real:
                    s = f.slot
                    e_inv.wait(dve, l, f)
                    v.scalar_tensor_tensor(out=enmi[:, s, :], in0=evar[:, s, :, 0], scalar=-1.0,
                                           in1=einv[:, s, :], op0=ALU.mult, op1=ALU.mult).then_inc(e_nmi.sem, 1)
                if e.real:
                    s = e.slot
                    gathered.wait(dve, l, e)
                    for w in range(NW):
                        last = v.bn_stats(estat[:, s, w, :], rows[:, s, w, 0:P])
                    last.then_inc(e_stats.sem, 1)
                    ep_in.wait(dve, l, e)
                    e_agg.wait(dve, l, e.back(SLOTS))
                    v.tensor_tensor(sel[:, s, 0:BATCH].rearrange("p (w j) -> p w j", w=NW), iota_win[:],
                                    edge_params(e, LOC).rearrange("p (w a) -> p w a", a=1)
                                    .to_broadcast([P, NW, WIN]), ALU.is_equal).then_inc(e_sel.sem, 1)
                    e_stats.wait(dve, l, e)
                    e_nmi.wait(dve, l, e.back(SLOTS))
                    e_std.wait(dve, l, e.back(SLOTS))
                    settle(dve, moved)
                    for w in range(NW):
                        last = v.bn_aggr(evar[:, s, w, :], estat[:, s, w, :])
                    last.then_inc(e_var.sem, 1)
                if old.real:
                    row_inverses(dve, l, old)
                    row_last(dve, l, old)
                if new.real:
                    row_stats(dve, l, new)

            def body12(t):
                new, summed, old, e, turned = t.back(4), t.back(5), t.back(6), t.back(2), t.back(3)
                if e.real:
                    s = e.slot
                    gathered.wait(dve, l, e)
                    ep_in.wait(dve, l, e)
                    v.tensor_tensor(scale[:, s, :], rows[:, s, 0:NW, INV], edge_params(e, DEG if l == 1 else EWT),
                                    ALU.mult).then_inc(e_scale.sem, 1)
                if summed.real:
                    row_means(dve, l, summed)
                if e.real:
                    e_agg.wait(dve, l, e.back(SLOTS))
                    for w in range(DVE_MSG[l]):
                        last = v.tensor_scalar(msg[:, s, w, :], rows[:, s, w, 0:P], rows[:, s, w, NMEAN:NMEAN + 1],
                                               0.0, ALU.add, ALU.max)
                    if l == 1:
                        last.then_inc(e_norm.sem, 1)
                    e_scale.wait(dve, l, e)
                    for w in range(NW):
                        last = v.tensor_scalar(sel[:, s, WIN * w:WIN * (w + 1)], iota_win[:, 0, :],
                                               edge_params(e, LOC + w, 1), scale[:, s, w:w + 1],
                                               ALU.is_equal, ALU.mult)
                    last.then_inc(e_sel.sem, 1)
                if new.real:
                    add_update(dve, l, new)
                if l == 2 and turned.real:
                    s = turned.slot
                    n_tr.wait(dve, l, turned)
                    n_aggt.wait(dve, l, turned)
                    n_mm.wait(dve, l, turned.back(SLOTS))
                    v.scalar_tensor_tensor(out=prod_t[:, s, :], in0=ps_t[:, 0:BATCH], scalar=0.0,
                                           in1=agg_t[:, s, :], op0=ALU.max, op1=ALU.mult).then_inc(n_prod.sem, 1)
                if old.real:
                    row_inverses(dve, l, old)
                if new.real:
                    row_stats(dve, l, new)
                if old.real:
                    row_last(dve, l, old)

            def body3(t):
                b = t.back(4)
                if b.real:
                    s = b.slot
                    e_eta.wait(dve, l, b)
                    n_mm.wait(dve, l, b.back(SLOTS))
                    v.tensor_tensor(msg[:, s], ps_o[:, 1, :].rearrange("p (w c) -> p w c", w=NW)[:, :, P:2 * P],
                                    eta[:, b.c % 2], ALU.mult).then_inc(e_msg.sem, 1)
                e = t.back(2)
                if e.real:
                    s = e.slot
                    gathered.wait(dve, l, e)
                    e_tr.wait(dve, l, e.back(SLOTS))
                    for w in range(NW):
                        last = v.tensor_scalar(eh[:, s, w, :], rows[:, s, w, 0:P], rows[:, s, w, INV:INV + 1],
                                               rows[:, s, w, NMI:NMI + 1], ALU.mult, ALU.add)
                    last.then_inc(e_norm.sem, 1)
                    ep_in.wait(dve, l, e)
                    n_mm.wait(dve, l, e.back(SLOTS))
                    for w in range(NW):
                        last = v.tensor_scalar(sel[:, s, 2 * P * w:2 * P * (w + 1)], iota_pair[:, w, :],
                                               edge_params(e, LOC + w, 1), None, ALU.is_equal)
                    last.then_inc(e_sel.sem, 1)
                if b.real:
                    add_update(dve, l, b)

            steps(dve, (7, 6, 6, 4)[l], (body0, body12, body12, body3)[l])

        def sums_psum(l, b):
            return ps_t if l == 0 and b.c % 2 else ps_e

        def act_layer(act, l):
            a = nc.scalar

            def new_std(b):
                n_var.wait(act, l, b)
                n_inv.wait(act, l, b.back(SLOTS))
                a.activation(std[:, b.slot, :], var[:, b.slot, :, 1], ACT.Sqrt, bias=eps_col[:]
                             ).then_inc(n_std.sem, 1)
                if l == 2:
                    x_stored.wait(act, l, b.back(SLOTS))
                    a.activation(xo[:, b.slot, :, NMEAN], var[:, b.slot, :, 0], ACT.Identity, scale=-1.0
                                 ).then_inc(n_mean.sem, 1)

            def normalise_nodes(b):
                s = b.slot
                x_in.wait(act, l, b)
                n_tr.wait(act, l, b.back(SLOTS))
                for r in range(NT):
                    last = a.activation(xh[:, s, r, :], xn[:, s, r, 0:P], ACT.Identity,
                                        bias=xn[:, s, r, NMI:NMI + 1], scale=xn[:, s, r, INV:INV + 1])
                last.then_inc(n_norm.sem, 1)

            def take_aggregate(b):
                s = b.slot
                e_agg.wait(act, l, b)
                n_mm.wait(act, l, b.back(SLOTS))
                a.copy(agg_t[:, s, :].rearrange("p (w j) -> p w j", w=NW),
                       sums_psum(l, b)[:].rearrange("p (w j) -> p w j", w=NW)[:, :, 0:WIN]).then_inc(n_aggt.sem, 1)

            def take_nodes(b):
                s = b.slot
                n_tr.wait(act, l, b)
                n_mm.wait(act, l, b.back(SLOTS))
                a.activation(h_t[:, s, :], ps_t[:, 0:BATCH], ACT.Relu).then_inc(n_ht.sem, 1)

            def body0(t):
                b = t.back(3)
                if b.real:
                    s = b.slot
                    e_nmi.wait(act, l, b)
                    gathered.wait(act, l, b)
                    e_agg.wait(act, l, b.back(SLOTS))
                    for w in range(NW):
                        last = a.activation(msg[:, s, w, :], rows[:, s, w, 0:P], ACT.Relu,
                                            bias=enmi[:, s, w:w + 1], scale=einv[:, s, w:w + 1])
                    last.then_inc(e_norm.sem, 1)
                b = t.back(5)
                if b.real:
                    n_mm.wait(act, l, b)
                    x_stored.wait(act, l, b.back(SLOTS))
                    a.copy(xo[:, b.slot, :, 0:P], update(l, b)).then_inc(n_out.sem, 1)
                b = t.back(4)
                if b.real:
                    take_aggregate(b)
                b = t.back(6)
                if b.real:
                    new_std(b)
                b = t.back(2)
                if b.real:
                    e_var.wait(act, l, b)
                    e_inv.wait(act, l, b.back(SLOTS))
                    a.activation(estd[:, b.slot, :], evar[:, b.slot, :, 1], ACT.Sqrt, bias=eps_col[:]
                                 ).then_inc(e_std.sem, 1)

            def body12(t):
                b = t.back(4)
                if l == 1 and b.real:
                    take_nodes(b)
                b = t.back(2)
                if b.real:
                    s = b.slot
                    gathered.wait(act, l, b)
                    e_agg.wait(act, l, b.back(SLOTS))
                    for w in range(DVE_MSG[l], NW):
                        last = a.activation(msg[:, s, w, :], rows[:, s, w, 0:P], ACT.Relu,
                                            bias=rows[:, s, w, NMEAN:NMEAN + 1])
                    last.then_inc(e_normd.sem, 1)
                b = t.back(3)
                if b.real:
                    take_aggregate(b)
                b = t.back(5)
                if b.real:
                    new_std(b)
                b = t.back(2)
                if b.real:
                    normalise_nodes(b)

            def body3(t):
                b = t.back(4)
                if b.real:
                    e_gate.wait(act, l, b)
                    e_msg.wait(act, l, b.back(2))
                    a.activation(eta[:, b.c % 2], ps_o[:, 1, :].rearrange("p (w c) -> p w c", w=NW)[:, :, 0:P],
                                 ACT.Sigmoid).then_inc(e_eta.sem, 1)
                b = t.back(2)
                if b.real:
                    normalise_nodes(b)
                b = t.back(3)
                if b.real:
                    e_tr.wait(act, l, b)
                    e_gate.wait(act, l, b.back(2))
                    a.activation(eh_t[:, b.c % 2], ps_e[:].rearrange("p (w c) -> p w c", c=P), ACT.Relu
                                 ).then_inc(e_ht.sem, 1)
                    take_nodes(b)
                b = t.back(2)
                if b.real:
                    s = b.slot
                    gathered.wait(act, l, b)
                    e_tr.wait(act, l, b.back(SLOTS))
                    for w in range(NW, 2 * NW):
                        last = a.activation(eh[:, s, w, :], rows[:, s, w, 0:P], ACT.Identity,
                                            bias=rows[:, s, w, NMI:NMI + 1], scale=rows[:, s, w, INV:INV + 1])
                    last.then_inc(e_normd.sem, 1)

            steps(act, (6, 5, 5, 4)[l], (body0, body12, body12, body3)[l])

        def pe_layer(pe, l):
            def aggregate(b):
                s = b.slot
                if l < 2:
                    e_norm.wait(pe, l, b)
                if l:
                    e_normd.wait(pe, l, b)
                e_sel.wait(pe, l, b)
                n_aggt.wait(pe, l, b.back(1 if l else 2))
                for w in range(NW):
                    mm = pe.matmul(sums_psum(l, b)[:, 2 * P * w:2 * P * w + WIN], msg[:, s, w, :],
                                   sel[:, s, WIN * w:WIN * (w + 1)], start=True, stop=True)
                mm.then_inc(e_agg.sem, 1)

            def turn_nodes(b):
                n_norm.wait(pe, l, b)
                (n_prod if l == 2 else n_ht).wait(pe, l, b.back(1))
                for r in range(NT):
                    mm = pe.transpose(ps_t[:, P * r:P * (r + 1)], xh[:, b.slot, r, :], ident[:])
                mm.then_inc(n_tr.sem, 1)

            def start_with(b, bias):
                o = 0 if l == 3 else b.c % 2
                pe.matmul(ps_o[:, o, 0:4 * P], ones3[:], bias[:].rearrange("p q f -> p (q f)"),
                          start=True, stop=False, skip_group_check=True)
                pe.matmul(ps_o[:, o, 4 * P:BATCH], ones3[:], bias[:, 0, :],
                          start=True, stop=False, skip_group_check=True)

            def body012(t):
                first = t.back(4 if l == 0 else 3)
                if l and first.real:
                    aggregate(first)
                b = t.back(5 if l == 0 else 4)
                if b.real:
                    products(b)
                if l == 0 and first.real:
                    aggregate(first)
                if l and first.real:
                    turn_nodes(first)

            def products(b):
                s = b.slot
                if l:
                    n_aggt.wait(pe, l, b)
                if l == 1:
                    n_ht.wait(pe, l, b)
                if l == 2:
                    n_prod.wait(pe, l, b)
                n_out.wait(pe, l, b.back(2))
                if l == 0:
                    x_in.wait(pe, l, b)
                    if isinstance(b.n, int) and b.n == BATCHES - 1:
                        pe.wait_ge(x_tail, 16)
                if l < 2:
                    start_with(b, (bias0, bias1)[l])
                if l == 0:
                    for r in range(NT):
                        pe.matmul(ps_o[:, b.c % 2, P * r:P * (r + 1)], ident[:], xn[:, s, r, 0:P],
                                  start=False, stop=False, skip_group_check=True)
                if l == 0:
                    n_aggt.wait(pe, l, b)
                terms = {0: [(agg_t, w0t)], 1: [(h_t, wselft), (agg_t, wneit)], 2: [(agg_t, w1), (prod_t, w2)]}[l]
                for r in range(NT):
                    for k, (left, w) in enumerate(terms):
                        mm = pe.matmul(ps_o[:, b.c % 2, P * r:P * (r + 1)], left[:, s, P * r:P * (r + 1)], w[:],
                                       start=(l == 2 and k == 0), stop=(k == len(terms) - 1),
                                       skip_group_check=True)
                mm.then_inc(n_mm.sem, 1)

            def body3(t):
                e = t.back(3)
                if e.real:
                    s = e.slot
                    e_norm.wait(pe, l, e)
                    e_normd.wait(pe, l, e)
                    e_ht.wait(pe, l, e.back(1))
                    for w in range(2 * NW):
                        mm = pe.transpose(ps_e[:, P * w:P * (w + 1)], eh[:, s, w, :], ident[:])
                    mm.then_inc(e_tr.sem, 1)
                    turn_nodes(e)
                b = t.back(4)
                if b.real:
                    s = b.slot
                    n_out.wait(pe, l, b.back(1))
                    n_ht.wait(pe, l, b)
                    start_with(b, bias3)
                    for r in range(NT):
                        pe.matmul(ps_o[:, 0, P * r:P * (r + 1)], h_t[:, s, P * r:P * (r + 1)], wr[:],
                                  start=False, stop=False, skip_group_check=True)
                    e_sel.wait(pe, l, b)
                    e_msg.wait(pe, l, b)
                    for w in range(NW):
                        for k in range(2):
                            mm = pe.matmul(ps_o[:, 0, P * (w + k):P * (w + k + 1)],
                                           sel[:, s, P * (2 * w + k):P * (2 * w + k + 1)], msg[:, s, w, :],
                                           start=False, stop=(k == 0 or w == NW - 1), skip_group_check=True)
                    mm.then_inc(n_mm.sem, 1)
                if e.real:
                    e_ht.wait(pe, l, e)
                    e_msg.wait(pe, l, e.back(1))
                    for w in range(0, NW, 2):
                        pe.matmul(ps_o[:, 1, 2 * P * w:2 * P * (w + 2)], ones3[:],
                                  biase[:].rearrange("p q f -> p (q f)"), start=True, stop=False,
                                  skip_group_check=True)
                    for w in range(NW):
                        pe.matmul(ps_o[:, 1, 2 * P * w:2 * P * (w + 1)], eh_t[:, e.c % 2, w, :], wg_ws[:],
                                  start=False, stop=False, skip_group_check=True)
                        mm = pe.matmul(ps_o[:, 1, 2 * P * w:2 * P * w + P], eh_t[:, e.c % 2, NW + w, :], wg_rec[:],
                                       start=False, stop=True, skip_group_check=True)
                    mm.then_inc(e_gate.sem, 1)

            steps(pe, (5, 4, 4, 4)[l], body3 if l == 3 else body012)

        key_of = {0: 1, 1: 1, 2: 0, 3: 1}
        fetch = {0: (0,), 1: (0,), 2: (1,), 3: (0, 1)}

        def fetches(l, k):
            return 16 * TILES * sum(len(fetch[m]) for m in range(l - k, l)), 16 * len(fetch[l])

        class Steps:

            def __init__(self, eng, sem, base, per):
                self.eng, self.sem, self.base, self.per = eng, sem, base, per

            def turn(self, t):
                self.at, self.n = self.base + self.per * t, 0

            def __call__(self, ins):
                self.n += 1
                assert self.n <= self.per
                ins.then_inc(self.sem, 1)
                self.eng.wait_ge(self.sem, self.at + self.n)

        EDGE_STEPS = 13
        NODE_STEPS = 11

        def general_zero(eng, k):
            with eng.Fori(0, BATCHES) as t:
                eng.dma_start(sums[bass.ds(BATCH * t, BATCH), :].rearrange("(r p) c -> p r c", p=P),
                              g_zero[:].rearrange("p (r c) -> p r c", c=SUM)).then_inc(g_zeroed, 16)
            eng.dma_start(sums[TRASH:TRASH + P, :], g_zero[:, 0:SUM]).then_inc(g_zeroed, 16)
            eng.wait_ge(g_zeroed, 16 * (BATCHES + 1) * (k + 1))

        def sp_edges(sp, l, k):
            general_zero(sp, k)
            with sp.Fori(0, TILES) as t:
                sp.dma_start(g_edge[:], edges[:, bass.ds(t, 1), :].rearrange("p a c -> p (a c)")
                             ).then_inc(g_edge_in, 16)
                sp.wait_ge(g_added, 16 * TILES * k + 16 * t + 16)
                settle(sp, moved)

        def pool_edges(pool, l, k):
            pool.wait_ge(g_zeroed, 16 * (BATCHES + 1) * (k + 1))
            with pool.Fori(0, TILES) as t:
                pool.wait_ge(g_edge_in, 16 * TILES * k + 16 * t + 16)
                settle(pool, moved)
                for j, f in enumerate(fetch[l]):
                    nc.gpsimd.indirect_dma_start(
                        rows[0:CAP, 0, j, 0:P], None, nodes[l],
                        bass.IndirectOffsetOnAxis(ap=g_edge[:, f:f + 1], axis=0)).then_inc(g_rows_in, 16)
                pool.wait_ge(g_totald, TILES * k + t + 1)
                settle(pool, moved)
                nc.gpsimd.indirect_dma_start(
                    sums, bass.IndirectOffsetOnAxis(ap=g_to[:, 0:1], axis=0), g_total[:], None,
                    compute_op=ALU.add).then_inc(g_added, 16)
            pool.wait_ge(g_added, 16 * TILES * (k + 1))

        def dve_edges(dve, l, k):
            v = nc.vector
            then = Steps(dve, g_step, TILES * EDGE_STEPS * k, EDGE_STEPS)
            fetched, own = fetches(l, k)
            with dve.Fori(0, TILES) as t:
                then.turn(t)
                n = TILES * k + t + 1
                dve.wait_ge(g_edge_in, 16 * TILES * k + 16 * t + 16)
                then(v.tensor_copy(g_key[:], g_edge[:, key_of[l]:key_of[l] + 1]))
                v.tensor_scalar(g_diag[:], ident[0:CAP, 0:CAP], g_key[:], None, ALU.mult).then_inc(g_diagd, 1)
                dve.wait_ge(g_keys, n)
                then(v.tensor_scalar(g_same[:], ps_e[0:CAP, 0:CAP], g_key[:], None, ALU.is_equal))
                then(v.tensor_tensor(g_before[:], g_same[:], g_earlier[:], ALU.mult))
                then(v.tensor_reduce(g_prior[:], g_before[:], AX.X, ALU.max))
                then(v.tensor_tensor(g_tof[:], g_trash[:], g_key[:], ALU.subtract))
                then(v.scalar_tensor_tensor(out=g_tof[:], in0=g_tof[:], scalar=g_prior[:], in1=g_key[:],
                                            op0=ALU.mult, op1=ALU.add))
                then(v.tensor_copy(g_to[:], g_tof[:]))
                m = len(fetch[l])
                dve.wait_ge(g_rows_in, fetched + own * t + own)
                for j in range(m):
                    last = v.bn_stats(estat[0:CAP, 0, j, :], rows[0:CAP, 0, j, 0:P])
                then(last)
                settle(dve, moved)
                for j in range(m):
                    last = v.bn_aggr(evar[0:CAP, 0, j, :], estat[0:CAP, 0, j, :])
                last.then_inc(g_var, 1)
                dve.wait_ge(g_std, n)
                then(v.reciprocal(einv[0:CAP, 0, 0:m], estd[0:CAP, 0, 0:m]))
                then(v.scalar_tensor_tensor(out=enmi[0:CAP, 0, 0:m], in0=evar[0:CAP, 0, 0:m, 0], scalar=-1.0,
                                            in1=einv[0:CAP, 0, 0:m], op0=ALU.mult, op1=ALU.mult))
                for j in range(m):
                    last = v.tensor_scalar(eh[0:CAP, 0, j, :], rows[0:CAP, 0, j, 0:P], einv[0:CAP, 0, j:j + 1],
                                           enmi[0:CAP, 0, j:j + 1], ALU.mult, ALU.add)
                if l == 3:
                    last.then_inc(g_hd, 1)
                    dve.wait_ge(g_eta, t + 1)
                    v.tensor_tensor(g_msg[:, 0:P], ps_o[0:CAP, 1, P:2 * P], eta[0:CAP, 0, 0, :], ALU.mult
                                    ).then_inc(g_msgd, 1)
                else:
                    then(last)
                    w = g_edge[:, 2:3].bitcast(F32) if l == 2 else 1.0
                    v.tensor_scalar(g_msg[:, 0:P], eh[0:CAP, 0, 0, :], 0.0, w, ALU.max, ALU.mult
                                    ).then_inc(g_msgd, 1)
                dve.wait_ge(g_comb, n)
                v.tensor_copy(g_total[:], ps_e[0:CAP, 512:512 + SUM]).then_inc(g_totald, 1)
                while then.n < EDGE_STEPS:
                    then(v.memset(g_before[0:1, 0:1], 0.0))

        def act_edges(act, l, k):
            a = nc.scalar
            with act.Fori(0, TILES) as t:
                n = TILES * k + t + 1
                m = len(fetch[l])
                act.wait_ge(g_var, n)
                a.activation(estd[0:CAP, 0, 0:m], evar[0:CAP, 0, 0:m, 1], ACT.Sqrt, bias=eps_col[0:CAP, :]
                             ).then_inc(g_std, 1)
                if l == 3:
                    act.wait_ge(g_tr, t + 1)
                    a.activation(eh_t[:, 0, 0:2, 0:CAP], ps_t[:, 0:2 * P].rearrange("p (w c) -> p w c", c=P)[:, :, 0:CAP],
                                 ACT.Relu).then_inc(g_ht, 1)
                    act.wait_ge(g_gate, t + 1)
                    a.activation(eta[0:CAP, 0, 0, :], ps_o[0:CAP, 1, 0:P], ACT.Sigmoid).then_inc(g_eta, 1)

        def pe_edges(pe, l, k):
            with pe.Fori(0, TILES) as t:
                n = TILES * k + t + 1
                pe.wait_ge(g_diagd, n)
                pe.matmul(ps_e[0:CAP, 0:CAP], g_ones[:], g_diag[:], start=True, stop=True).then_inc(g_keys, 1)
                if l == 3:
                    pe.wait_ge(g_hd, t + 1)
                    for j in range(2):
                        mm = pe.transpose(ps_t[:, P * j:P * j + CAP], eh[0:CAP, 0, j, :], ident[0:CAP, 0:CAP])
                    mm.then_inc(g_tr, 1)
                    pe.wait_ge(g_ht, t + 1)
                    pe.matmul(ps_o[0:CAP, 1, 0:2 * P], ones3[:, 0:CAP], biase[:, 0:2, :].rearrange("p q f -> p (q f)"),
                              start=True, stop=False, skip_group_check=True)
                    pe.matmul(ps_o[0:CAP, 1, 0:2 * P], eh_t[:, 0, 0, 0:CAP], wg_ws[:],
                              start=False, stop=False, skip_group_check=True)
                    pe.matmul(ps_o[0:CAP, 1, 0:P], eh_t[:, 0, 1, 0:CAP], wg_rec[:],
                              start=False, stop=True, skip_group_check=True).then_inc(g_gate, 1)
                pe.wait_ge(g_msgd, n)
                pe.matmul(ps_e[0:CAP, 512:512 + SUM], g_same[:], g_msg[:], start=True, stop=True).then_inc(g_comb, 1)

        def per_batch(eng, body):
            with eng.Fori(0, BATCHES - 1) as t:
                body(t)
            body(BATCHES - 1)

        def sp_nodes(sp, l, k):
            def body(t):
                n = BATCHES * k + t
                last = isinstance(t, int)
                if l == 0 and last:
                    sp.dma_start(xn[:, 0, 0, 0:P], x[NODES - TAIL:NODES - TAIL + P, :]).then_inc(gn_in, 16)
                    sp.wait_ge(gn_in, 16 * n + 16)
                    sp.dma_start(xn[0:TAIL - P, 0, 1, 0:P], x[NODES - TAIL + P:NODES, :]).then_inc(x_tail, 16)
                else:
                    sp.dma_start(xn[:, 0, :, 0:P], node_rows(l, t)[:, :, 0:P]).then_inc(gn_in, 16)
                sp.dma_start(g_sums[:], sums[bass.ds(BATCH * t, BATCH), :].rearrange("(r p) c -> p r c", p=P)
                             ).then_inc(gn_sums_in, 16)
                sp.wait_ge(gn_out, n + 1)
                settle(sp, moved)
                if l < 3:
                    sp.dma_start(node_rows(l + 1, t), xo[:, 0]).then_inc(gn_stored, 16)
                elif last:
                    sp.dma_start(out[NODES - TAIL:NODES - TAIL + P, :], xo[:, 0, 0, 0:P]).then_inc(gn_stored, 16)
                    sp.dma_start(out[NODES - TAIL + P:NODES, :], xo[0:TAIL - P, 0, 1, 0:P]).then_inc(out_tail, 16)
                    sp.wait_ge(out_tail, 16)
                else:
                    sp.dma_start(out[bass.ds(BATCH * t, BATCH), :].rearrange("(r p) c -> p r c", p=P),
                                 xo[:, 0, :, 0:P]).then_inc(gn_stored, 16)
                sp.wait_ge(gn_stored, 16 * n + 16)
                settle(sp, moved)

            per_batch(sp, body)

        def dve_nodes(dve, l, k):
            v = nc.vector
            then = Steps(dve, gn_step, BATCHES * NODE_STEPS * k, NODE_STEPS)

            def body(t):
                then.turn(t)
                n = BATCHES * k + t + 1
                dve.wait_ge(gn_in, 16 * n)
                if l == 0 and isinstance(t, int):
                    dve.wait_ge(x_tail, 16)
                for again, x_rows in enumerate((xn, xo)):
                    for r in range(NT):
                        last = v.bn_stats(stat[:, 0, r, :], x_rows[:, 0, r, 0:P])
                    then(last)
                    settle(dve, moved)
                    for r in range(NT):
                        last = v.bn_aggr(var[:, 0, r, :], stat[:, 0, r, :])
                    last.then_inc(gn_var, 1)
                    dve.wait_ge(gn_std, 2 * n - 1 + again)
                    then(v.reciprocal(x_rows[:, 0, :, INV], std[:, 0, :]))
                    then(v.tensor_scalar(x_rows[:, 0, :, NMEAN], var[:, 0, :, 0], -1.0, None, ALU.mult))
                    last = v.tensor_tensor(x_rows[:, 0, :, NMI], x_rows[:, 0, :, NMEAN], x_rows[:, 0, :, INV], ALU.mult)
                    if again:
                        last.then_inc(gn_out, 1)
                        break
                    then(last)
                    for r in range(NT):
                        last = v.tensor_scalar(xh[:, 0, r, :], xn[:, 0, r, 0:P], xn[:, 0, r, INV:INV + 1],
                                               xn[:, 0, r, NMI:NMI + 1], ALU.mult, ALU.add)
                    dve.wait_ge(gn_sums_in, 16 * n)
                    if l == 1:
                        then(v.tensor_scalar(g_deg[:], g_sums[:, :, P], 1.0, None, ALU.max))
                        then(v.reciprocal(g_deg[:], g_deg[:]))
                        for r in range(NT):
                            last = v.tensor_scalar(g_mean[:, r, :], g_sums[:, r, 0:P], g_deg[:, r:r + 1], None, ALU.mult)
                    else:
                        last = v.tensor_copy(g_mean[:], g_sums[:, :, 0:P])
                    last.then_inc(gn_ready, 1)
                    if l == 2:
                        dve.wait_ge(gn_take, n)
                        v.tensor_tensor(prod_t[:, 0, :], agg_t[:, 0, :], h_t[:, 0, :], ALU.mult).then_inc(gn_prod, 1)
                    dve.wait_ge(gn_mm, n)
                    add_to = xn[:, 0, :, 0:P]
                    if l == 3:
                        then(v.tensor_tensor(g_mean[:], g_mean[:], xn[:, 0, :, 0:P], ALU.add))
                        add_to = g_mean[:]
                    new = ps_o[:, 0, 0:BATCH].rearrange("p (r f) -> p r f", f=P)
                    if l == 1:
                        then(v.scalar_tensor_tensor(out=xo[:, 0, :, 0:P], in0=new, scalar=0.0, in1=add_to,
                                                    op0=ALU.max, op1=ALU.add))
                    else:
                        then(v.tensor_tensor(xo[:, 0, :, 0:P], new, add_to, ALU.add))
                while then.n < NODE_STEPS:
                    then(v.memset(g_deg[0:1, 0:1], 0.0))

            per_batch(dve, body)

        def act_nodes(act, l, k):
            a = nc.scalar

            def body(t):
                n = BATCHES * k + t + 1
                act.wait_ge(gn_var, 2 * n - 1)
                a.activation(std[:, 0, :], var[:, 0, :, 1], ACT.Sqrt, bias=eps_col[:]).then_inc(gn_std, 1)
                act.wait_ge(gn_tr, n)
                a.copy(agg_t[:, 0, :], ps_e[:, 0:BATCH])
                a.activation(h_t[:, 0, :], ps_t[:, 0:BATCH], ACT.Relu).then_inc(gn_take, 1)
                act.wait_ge(gn_var, 2 * n)
                a.activation(std[:, 0, :], var[:, 0, :, 1], ACT.Sqrt, bias=eps_col[:]).then_inc(gn_std, 1)

            per_batch(act, body)

        def pe_nodes(pe, l, k):
            def body(t):
                n = BATCHES * k + t + 1
                pe.wait_ge(gn_ready, n)
                for r in range(NT):
                    pe.transpose(ps_e[:, P * r:P * (r + 1)], g_mean[:, r, :], ident[:])
                for r in range(NT):
                    mm = pe.transpose(ps_t[:, P * r:P * (r + 1)], xh[:, 0, r, :], ident[:])
                mm.then_inc(gn_tr, 1)
                pe.wait_ge(gn_take, n)
                bias = (bias0, bias1, None, bias3)[l]
                if l == 2:
                    pe.wait_ge(gn_prod, t + 1)
                else:
                    pe.matmul(ps_o[:, 0, 0:4 * P], ones3[:], bias[:].rearrange("p q f -> p (q f)"),
                              start=True, stop=False, skip_group_check=True)
                    pe.matmul(ps_o[:, 0, 4 * P:BATCH], ones3[:], bias[:, 0, :],
                              start=True, stop=False, skip_group_check=True)
                terms = {0: [(agg_t, w0t)], 1: [(h_t, wselft), (agg_t, wneit)], 2: [(agg_t, w1), (prod_t, w2)],
                         3: [(h_t, wr)]}[l]
                for r in range(NT):
                    for j, (left, w) in enumerate(terms):
                        mm = pe.matmul(ps_o[:, 0, P * r:P * (r + 1)], left[:, 0, P * r:P * (r + 1)], w[:],
                                       start=(l == 2 and j == 0), stop=(j == len(terms) - 1), skip_group_check=True)
                mm.then_inc(gn_mm, 1)

            per_batch(pe, body)

        block = ctx.enter_context(nc.Block())

        def program(eng, prepare, layer, edges_pass, nodes_pass):
            prepare(eng)
            join(eng, 1)
            general = eng.value_load(flag[0:1, 0:1], min_val=0, max_val=1)
            with eng.If(general > 0):
                for l in range(4):
                    edges_pass(eng, l, l)
                    join(eng, 2 + 2 * l)
                    nodes_pass(eng, l, l)
                    join(eng, 3 + 2 * l)
            with eng.Else():
                for l in range(4):
                    layer(eng, l)
                    join(eng, 2 + l)

        def nothing(eng, l, k):
            pass

        @block.sync
        def _(sp):
            program(sp, sp_prepare, sp_layer, sp_edges, sp_nodes)

        @block.gpsimd
        def _(pool):
            program(pool, pool_prepare, pool_layer, pool_edges, nothing)

        @block.scalar
        def _(act):
            program(act, act_prepare, act_layer, act_edges, act_nodes)

        @block.tensor
        def _(pe):
            program(pe, pe_prepare, pe_layer, pe_edges, pe_nodes)

        @block.vector
        def _(dve):
            program(dve, dve_prepare, dve_layer, dve_edges, dve_nodes)


_INS = ["x", "src", "dst", "edge_weight", "L0_gnn_W", "L0_gnn_b", "L1_gnn_W_self", "L1_gnn_b_self",
        "L1_gnn_W_nei", "L1_gnn_b_nei", "L2_gnn_W1", "L2_gnn_W2", "L3_gnn_Wg", "L3_gnn_bg", "L3_gnn_Ws",
        "L3_gnn_bs", "L3_gnn_Wr", "L3_gnn_br"]


def kernel(**inputs):
    import concourse.bacc as bacc
    from concourse.bass_utils import run_bass_kernel_spmd

    nc = bacc.Bacc("TRN2", target_bir_lowering=False, num_devices=1)
    arrays, args = {}, []
    for name in _INS:
        a = np.ascontiguousarray(inputs[name])
        arrays[f"in_{name}"] = a
        args.append(nc.dram_tensor(f"in_{name}", a.shape, mybir.dt.from_np(a.dtype), kind="ExternalInput").ap())
    args.append(nc.dram_tensor("out_x", (NODES, P), F32, kind="ExternalOutput").ap())
    build(nc, *args)
    r = run_bass_kernel_spmd(nc, [arrays], core_ids=[0])
    return r.results[0]["out_x"]
```
